# Optimizing a Trainium2 kernel written in Bass

```python
import numpy as np
import jax
import jax.numpy as jnp

def _softmax(x, axis=-1):
    return jax.nn.softmax(x, axis=axis)

def _gelu(x):
    return jax.nn.gelu(x, approximate=True)

def _silu(x):
    return jax.nn.silu(x)

def _sigmoid(x):
    return jax.nn.sigmoid(x)

def _layernorm(x, axis=-1, eps=1e-05):
    m = jnp.mean(x, axis=axis, keepdims=True)
    v = jnp.var(x, axis=axis, keepdims=True)
    return (x - m) / jnp.sqrt(v + eps)

def _scatter_add(tgt, idx, src, axis=0):
    return tgt.at[idx].add(src)

def _segment_sum(src, seg, n):
    return jax.ops.segment_sum(src, seg, n)
kernel_name = 'mk_perceiver_d1_seqx_r4_761e1c'

def setup_inputs(seed: int=0):
    np.random.seed(seed)
    _w = jnp.asarray

    def _rec_inputs():
        import jax
        import jax.numpy as jnp
        _rk = jax.random.key(seed)
        x = -0.0002928 + 1 * jax.random.normal(jax.random.fold_in(_rk, 1), (2, 256, 256), jnp.float32)
        _lenS = 256 - jax.random.randint(jax.random.fold_in(_rk, 7), (2,), 0, max(1, 256 // 4) + 1, jnp.int32)
        _lenS2 = 4096 - jax.random.randint(jax.random.fold_in(_rk, 8), (2,), 0, max(1, 4096 // 4) + 1, jnp.int32)
        _ctx_1024P = jax.random.normal(jax.random.fold_in(_rk, 11), (2, 16, 256), jnp.float32)
        _ctx_1024c = jax.random.dirichlet(jax.random.fold_in(_rk, 511), 0.3 * jnp.ones((16,), jnp.float32), (2, 4096))
        _ctx_1024t = jnp.einsum('bsk,bkd->bsd', _ctx_1024c, _ctx_1024P)
        _ctx_1024t = _ctx_1024t * jax.lax.rsqrt(jnp.mean(jnp.square(_ctx_1024t)) + 1e-12) * 0.953939
        ctx_1024 = -1.39393e-06 + 0.999914 * (_ctx_1024t + 0.3 * jax.random.normal(jax.random.fold_in(_rk, 611), (2, 4096, 256), jnp.float32))
        return (x, ctx_1024)
    x, ctx_1024 = _rec_inputs()

    def _L0_xattn_setup():
        import jax, jax.numpy as jnp
        import numpy as np
        D_MODEL = 256
        N_HEAD = 16
        D_HEAD = D_MODEL // N_HEAD
        key = jax.random.key(seed)
        ks = jax.random.split(key, 6)
        B, L, M = (2, 512, 512)
        q = jax.random.normal(ks[0], (B, L, D_MODEL), dtype=jnp.float32)
        kv = jax.random.normal(ks[1], (B, L, D_MODEL), dtype=jnp.float32)
        mem = jax.random.normal(ks[2], (B, M, D_MODEL), dtype=jnp.float32)
        s = 1.0 / np.sqrt(D_MODEL)
        w_q = jax.random.normal(ks[3], (D_MODEL, D_MODEL), dtype=jnp.float32) * s
        w_kv = jax.random.normal(ks[4], (D_MODEL, 2 * D_HEAD), dtype=jnp.float32) * s
        w_concat = jax.random.normal(ks[5], (D_MODEL, D_MODEL), dtype=jnp.float32) * s
        return {'q': q, 'kv': kv, 'mem': mem, 'w_q': w_q, 'w_kv': w_kv, 'w_concat': w_concat}
    _L0_xattn_all = _L0_xattn_setup()
    _L0_xattn_in = {k: v for k, v in _L0_xattn_all.items() if k in ('w_q', 'w_kv', 'w_concat')}
    del _L0_xattn_all

    def _L0_attn_setup():
        import jax, jax.numpy as jnp
        import numpy as np
        N, L, D_IN, H, HD, D_OUT = (4, 512, 256, 16, 64, 256)
        DIM = H * HD
        key = jax.random.key(seed)
        ks = jax.random.split(key, 5)
        s_in = 1.0 / np.sqrt(D_IN)
        s_d = 1.0 / np.sqrt(DIM)
        return {'data': jax.random.normal(ks[0], (N, L, D_IN), jnp.float32), 'W_qkv': jax.random.uniform(ks[1], (D_IN, 3 * DIM), jnp.float32, -s_in, s_in), 'b_qkv': jax.random.uniform(ks[2], (3 * DIM,), jnp.float32, -s_in, s_in), 'W_out': jax.random.uniform(ks[3], (DIM, D_OUT), jnp.float32, -s_d, s_d), 'b_out': jax.random.uniform(ks[4], (D_OUT,), jnp.float32, -s_d, s_d)}
    _L0_attn_all = _L0_attn_setup()
    _L0_attn_in = {k: v for k, v in _L0_attn_all.items() if k in ('W_qkv', 'b_qkv', 'W_out', 'b_out')}
    del _L0_attn_all

    def _L0_ffn_setup():
        import jax, jax.numpy as jnp
        import numpy as np
        E = 16
        K = 4
        NG = 4
        TG = 2
        SCALE = 2.5
        NORM_TOPK = True
        H = 256
        I = 128
        SH_I = I * 2
        B, S = (2, 512)
        key = jax.random.key(seed)
        ks = jax.random.split(key, 9)

        def w(k, shape, fan_in):
            return jax.random.normal(k, shape, jnp.float32) * (1.0 / np.sqrt(fan_in))
        return {'hidden_states': jax.random.normal(ks[0], (B, S, H), jnp.float32), 'gate_w': w(ks[1], (E, H), H), 'gate_bias': jnp.zeros((E,), jnp.float32), 'Wg': w(ks[2], (E, I, H), H), 'Wu': w(ks[3], (E, I, H), H), 'Wd': w(ks[4], (E, H, I), I), 'Ws_g': w(ks[5], (SH_I, H), H), 'Ws_u': w(ks[6], (SH_I, H), H), 'Ws_d': w(ks[7], (H, SH_I), SH_I)}
    _L0_ffn_all = _L0_ffn_setup()
    _L0_ffn_in = {k: v for k, v in _L0_ffn_all.items() if k in ('gate_w', 'gate_bias', 'Wg', 'Wu', 'Wd', 'Ws_g', 'Ws_u', 'Ws_d')}
    del _L0_ffn_all
    return {'x': x, 'ctx_1024': ctx_1024, 'L0_xattn_w_q': _L0_xattn_in['w_q'], 'L0_xattn_w_kv': _L0_xattn_in['w_kv'], 'L0_xattn_w_concat': _L0_xattn_in['w_concat'], 'L0_attn_W_qkv': _L0_attn_in['W_qkv'], 'L0_attn_b_qkv': _L0_attn_in['b_qkv'], 'L0_attn_W_out': _L0_attn_in['W_out'], 'L0_attn_b_out': _L0_attn_in['b_out'], 'L0_ffn_gate_w': _L0_ffn_in['gate_w'], 'L0_ffn_gate_bias': _L0_ffn_in['gate_bias'], 'L0_ffn_Wg': _L0_ffn_in['Wg'], 'L0_ffn_Wu': _L0_ffn_in['Wu'], 'L0_ffn_Wd': _L0_ffn_in['Wd'], 'L0_ffn_Ws_g': _L0_ffn_in['Ws_g'], 'L0_ffn_Ws_u': _L0_ffn_in['Ws_u'], 'L0_ffn_Ws_d': _L0_ffn_in['Ws_d']}

def reference(x, ctx_1024, L0_xattn_w_q, L0_xattn_w_kv, L0_xattn_w_concat, L0_attn_W_qkv, L0_attn_b_qkv, L0_attn_W_out, L0_attn_b_out, L0_ffn_gate_w, L0_ffn_gate_bias, L0_ffn_Wg, L0_ffn_Wu, L0_ffn_Wd, L0_ffn_Ws_g, L0_ffn_Ws_u, L0_ffn_Ws_d):
    import jax
    import jax.numpy as jnp

    def _L0_xattn_ref(q, kv, mem, w_q, w_kv, w_concat):
        import jax, jax.numpy as jnp
        import numpy as np
        D_MODEL = 256
        N_HEAD = 16
        D_HEAD = D_MODEL // N_HEAD
        B, L, D = q.shape
        c = jnp.concatenate([mem, kv], axis=1)
        qh = (q @ w_q).reshape(B, L, N_HEAD, D_HEAD).transpose(0, 2, 1, 3)
        kvp = c @ w_kv
        k, v = (kvp[..., :D_HEAD], kvp[..., D_HEAD:])
        attn_score = jnp.einsum('bhid,bjd->bhij', qh, k) / np.sqrt(D_HEAD)
        attn_prob = jax.nn.softmax(attn_score, axis=-1)
        out = jnp.einsum('bhij,bjd->bhid', attn_prob, v)
        out = out.transpose(0, 2, 1, 3).reshape(B, L, D)
        return out @ w_concat

    def _L0_attn_ref(data, W_qkv, b_qkv, W_out, b_out):
        import jax, jax.numpy as jnp
        import numpy as np
        N, L, D_IN, H, HD, D_OUT = (4, 512, 256, 16, 64, 256)
        DIM = H * HD
        n, l = (data.shape[0], data.shape[1])
        qkv = data @ W_qkv + b_qkv
        q = qkv[:, :, :DIM].reshape(n, l, H, HD)
        k = qkv[:, :, DIM:2 * DIM].reshape(n, l, H, HD)
        v = qkv[:, :, 2 * DIM:].reshape(n, l, H, HD)
        scores = jnp.einsum('nqhd,nkhd->nhqk', q, k)
        attention = jax.nn.softmax(scores / jnp.sqrt(jnp.float32(HD)), axis=3)
        out = jnp.einsum('nhql,nlhd->nqhd', attention, v).reshape(n, l, DIM)
        return out @ W_out + b_out

    def _L0_ffn_ref(hidden_states, gate_w, gate_bias, Wg, Wu, Wd, Ws_g, Ws_u, Ws_d):
        import jax, jax.numpy as jnp
        import numpy as np
        E = 16
        K = 4
        NG = 4
        TG = 2
        SCALE = 2.5
        NORM_TOPK = True
        H = 256
        I = 128
        SH_I = I * 2
        B, S = (2, 512)
        x = hidden_states
        b, s, h = x.shape
        n = b * s
        xf = x.reshape(n, h)
        logits = xf @ gate_w.T
        scores = jax.nn.sigmoid(logits)
        sfc = scores + gate_bias
        epg = E // NG
        grp = sfc.reshape(n, NG, epg)
        g_scores = jax.lax.top_k(grp, 2)[0].sum(-1)
        _, gidx = jax.lax.top_k(g_scores, TG)
        gmask = jax.nn.one_hot(gidx, NG, dtype=sfc.dtype).sum(1)
        emask = jnp.repeat(gmask, epg, axis=1)
        masked = jnp.where(emask > 0, sfc, -jnp.inf)
        _, topk_idx = jax.lax.top_k(masked, K)
        topk_w = jnp.take_along_axis(scores, topk_idx, axis=1)
        if K > 1 and NORM_TOPK:
            topk_w = topk_w / (topk_w.sum(-1, keepdims=True) + 1e-20)
        topk_w = topk_w * SCALE
        cw = (jax.nn.one_hot(topk_idx, E, dtype=topk_w.dtype) * topk_w[..., None]).sum(1)
        hg = jnp.einsum('nh,eih->nei', xf, Wg)
        hu = jnp.einsum('nh,eih->nei', xf, Wu)
        act = jax.nn.silu(hg) * hu
        y = jnp.einsum('nei,ne,ehi->nh', act, cw, Wd)
        shared = jax.nn.silu(xf @ Ws_g.T) * (xf @ Ws_u.T) @ Ws_d.T
        y = y + shared
        return (x + y.reshape(b, s, h)).astype(hidden_states.dtype)
    x = x + _L0_xattn_ref(_layernorm(x, axis=-1), ctx_1024, ctx_1024, L0_xattn_w_q, L0_xattn_w_kv, L0_xattn_w_concat)
    x = x + _L0_attn_ref(_layernorm(x, axis=-1), L0_attn_W_qkv, L0_attn_b_qkv, L0_attn_W_out, L0_attn_b_out)
    x = x + _L0_ffn_ref(_layernorm(x, axis=-1), L0_ffn_gate_w, L0_ffn_gate_bias, L0_ffn_Wg, L0_ffn_Wu, L0_ffn_Wd, L0_ffn_Ws_g, L0_ffn_Ws_u, L0_ffn_Ws_d)
    return x

_drawn_inputs = setup_inputs


def setup_inputs(seed=0):
    import zlib

    import numpy as np

    out = dict(_drawn_inputs(seed))
    spreads = {'L0_ffn_gate_bias': (0.0, 0.1)}
    factors = {}
    for name, (base, spread) in spreads.items():
        noise = np.random.default_rng([zlib.crc32(name.encode()), seed]).standard_normal(out[name].shape)
        drawn = base * np.exp(spread * noise) if base else spread * noise
        out[name] = jnp.asarray(drawn.astype(out[name].dtype))
    for name, factor in factors.items():
        out[name] = (out[name] * factor).astype(out[name].dtype)
    return out
```

```python
from contextlib import ExitStack

import numpy as np

import concourse.bass as bass
from concourse import mybir

ALU = mybir.AluOpType
ACT = mybir.ActivationFunctionType
AX = mybir.AxisListType.X
F32 = mybir.dt.float32
BF16 = mybir.dt.bfloat16
I32 = mybir.dt.int32

P = 128
B, L, D = 2, 256, 256
S = 4096
T = B * L // P
KD = D // P
XH, XD = 16, 16
NP6 = 6
XK = NP6 * XD
MR = 3
KT = S // P
CW = 512
NCH = XH * L // CW
NBLK = CW // P
KC = S // 512
AHEAD = NBLK + 1
QUADS = KT // 4
VW = 32
AH, AD = 16, 64
DIM = AH * AD
NPAIR = AH // 2
AW = KD * 3 * P + D + 3
E, I = 16, 128
NE = E + 2
EW = KD * 2 * P + D
NG, TG, TOPK = 4, 2, 4
EPS = 1e-5
RSQRT_MAGIC = float(0x5F3759DF)
BIG = 3.0e38

Q_PART = [1, 2, 1, 2, 3, 1]
K_PART = [1, 1, 2, 2, 1, 3]


class Chain:

    def __init__(self, eng, sem):
        self.eng, self.sem, self.n, self.extra = eng, sem, 0, 0

    def loop(self, turn, per):
        self.start, self.per, self.extra = self.n, per, turn * per

    def end(self, turns):
        assert self.n - self.start == self.per, (self.n - self.start, self.per)
        self.n += self.per * (turns - 1)
        self.extra = 0

    def step(self, ins):
        self.n += 1
        ins.then_inc(self.sem, 1)
        self.eng.wait_ge(self.sem, self.extra + self.n)


def build(nc, x, ctxT, w_q, w_kv, w_cat, w_attn, b_out, gate_wT, gate_b, w_exp, out):
    with ExitStack() as stack:
        def sb(name, shape, dt=F32):
            return stack.enter_context(nc.sbuf_tensor(name, shape, dt))

        def sem(name):
            return stack.enter_context(nc.semaphore(name))

        bank = [stack.enter_context(nc.psum_tensor(f"bank{i}", [P, 512], F32)) for i in range(4)]
        pairS = [stack.enter_context(nc.psum_tensor(f"pairS{i}", [P, 1024], F32)) for i in range(2)]
        XB = [bank[0], bank[1]]
        ACC = bank[2]
        MISC = bank[3]
        half = [pairS[0][:, 0:512], pairS[0][:, 512:1024], pairS[1][:, 0:512], pairS[1][:, 512:1024]]

        ident = sb("ident", [P, P])
        identb = sb("identb", [P, P], BF16)
        xs = sb("xs", [P, T, D])
        xn = sb("xn", [P, T, D])
        xnT = sb("xnT", [P, KD, B * L])
        st6 = sb("st6", [P, T, 6])
        mv = sb("mv", [P, T, 2])
        rv = sb("rv", [P, T])
        ry = sb("ry", [P, T])
        rt = sb("rt", [P, T])
        wq = sb("wq", [P, KD, D])
        wkv = sb("wkv", [P, KD, 2 * XD])
        wcat = sb("wcat", [P, KD, D])
        ctx = [sb(f"ctx{b}", [P, KD, S]) for b in range(B)]
        kvT = sb("kvT", [P, 2, 512])
        kraw = sb("kraw", [P, KT // 2, XD])
        res = sb("res", [P, 64 * XD])
        kasm = sb("kasm", [P, KT // 2, XK], BF16)
        qasm = sb("qasm", [P, 2 * XH * 2, XK], BF16)
        kparts = [sb(f"kparts{b}", [XK + MR, S], BF16) for b in range(B)]
        qparts = sb("qparts", [XK + MR, B * XH * L], BF16)
        V = [sb(f"V{b}", [P, KT, VW]) for b in range(B)]
        Pb = sb("Pb", [P, 4, 1024])
        mxp = sb("mxp", [P, NBLK, KC])
        negm = sb("negm", [P, NBLK])
        mres = sb("mres", [P, NBLK])
        mparts = sb("mparts", [P, NBLK, MR], BF16)
        accS = sb("accS", [P, 512])
        osum = sb("osum", [P, NBLK, XD + 1])
        oden = sb("oden", [P, NBLK])
        O = sb("O", [P, T, D])

        wA = [sb(f"wA{i}", [P, AW]) for i in range(2)]
        qz = [sb(f"qz{i}", [P, 2, B * L]) for i in range(2)]
        kTb = [sb(f"kTb{i}", [P, B * L]) for i in range(2)]
        vTb = sb("vTb", [P, B * L])
        vn = [sb(f"vn{i}", [P, T, P]) for i in range(2)]
        smx = sb("smx", [P, 4, 2])
        snb = sb("snb", [P, 4, 2])
        sden = sb("sden", [P, 4, 2])
        srd = sb("srd", [P, 4, 2])
        bo2 = sb("bo2", [1, 2, D])
        one_row = sb("one_row", [1, P])
        wE = [sb(f"wE{i}", [P, EW]) for i in range(2)]
        gwT = sb("gwT", [P, KD, E])
        gb = sb("gb", [P, E])
        cw = sb("cw", [P, T, NE])
        sp_ = Pb[:, 0:2, :].rearrange("p a (c k) -> p (a c) k", k=512)
        spT = Pb[:, 2, :].rearrange("p (a k) -> p a k", a=2)
        aT = Pb[:, 3, 0:512]
        hsil = [Pb[:, 0, 0:512], Pb[:, 0, 512:1024]]
        hT = [Pb[:, 1, 0:512], Pb[:, 1, 512:1024]]

        x_in, wq_in, wkv_in = sem("x_in"), sem("wq_in"), sem("wkv_in")
        late_in = sem("late_in")
        ctx_in = [[sem(f"ctx_in{b}{s}") for s in range(2)] for b in range(B)]
        wA_in = [sem("wA_in0"), sem("wA_in1")]
        wE_in = [sem("wE_in0"), sem("wE_in1")]
        out_done = sem("out_done")
        ident_done, const_done = sem("ident_done"), sem("const_done")
        dve_chain, act_chain, pool_chain = sem("dve_chain"), sem("act_chain"), sem("pool_chain")
        ln_done, xnT_ps, xnT_done = sem("ln_done"), sem("xnT_ps"), sem("xnT_done")
        q_ps, q_asm, qt_ps, qt_done = sem("q_ps"), sem("q_asm"), sem("qt_ps"), sem("qt_done")
        kv_ps, kvT_done, kn_ps, kn_read = sem("kv_ps"), sem("kvT_done"), sem("kn_ps"), sem("kn_read")
        k_asm, kt_ps, kt_done = sem("k_asm"), sem("kt_ps"), sem("kt_done")
        xmax_ready, xmax_read = sem("xmax_ready"), sem("xmax_read")
        mparts_ready, mrows_ps, mrows_ready = sem("mparts_ready"), sem("mrows_ps"), sem("mrows_ready")
        scores_ready, exp_done, pv_done = sem("scores_ready"), sem("exp_done"), sem("pv_done")
        acc_saved, accT_ps, accT_read = sem("acc_saved"), sem("accT_ps"), sem("accT_read")
        o_done, oT_ps, oT_done, y_ps = sem("o_done"), sem("oT_ps"), sem("oT_done"), sem("y_ps")
        proj_ps, q_moved, k_moved, v_moved = sem("proj_ps"), sem("q_moved"), sem("k_moved"), sem("v_moved")
        vn_ps, vn_done = sem("vn_ps"), sem("vn_done")
        s_ps, s_max, s_exp, s_norm = sem("s_ps"), sem("s_max"), sem("s_exp"), sem("s_norm")
        pT_ps, pT_done, av_ps, aT_done, ao_ps = sem("pT_ps"), sem("pT_done"), sem("av_ps"), sem("aT_done"), sem("ao_ps")
        wA_used = sem("wA_used")
        gate_ps, cw_done, gate_exp = sem("gate_ps"), sem("cw_done"), sem("gate_exp")
        up_ps, sil_done, hT_done, down_ps, down_read = (sem("up_ps"), sem("sil_done"), sem("hT_done"),
                                                        sem("down_ps"), sem("down_read"))

        x_dram = x.rearrange("b (t p) d -> p (b t) d", p=P)
        out_dram = out.rearrange("b (t p) d -> p (b t) d", p=P)

        block = stack.enter_context(nc.Block())

        @block.sync
        def _(sp):
            sp.dma_start(xs[:], x_dram).then_inc(x_in, 16)
            for b in range(B):
                for s in range(2):
                    c = slice(s * S // 2, (s + 1) * S // 2)
                    sp.dma_start(ctx[b][:, :, c], ctxT[b].rearrange("(k p) s -> p k s", p=P)[:, :, c]
                                 ).then_inc(ctx_in[b][s], 16)
            sp.dma_start(wcat[:], w_cat.rearrange("(k p) n -> p k n", p=P)).then_inc(late_in, 16)
            sp.dma_start(gwT[:], gate_wT.rearrange("(k p) n -> p k n", p=P)).then_inc(late_in, 16)
            for i in range(2):
                sp.dma_start(wA[i][:], w_attn[i]).then_inc(wA_in[i], 16)
            for i in range(2):
                sp.dma_start(wE[i][:], w_exp[i]).then_inc(wE_in[i], 16)
            for j in range(2):
                sp.dma_start(bo2[:, j, :], b_out.rearrange("(o n) -> o n", o=1)).then_inc(late_in, 16)
            sp.dma_start(gb[:], gate_b.rearrange("(o n) -> o n", o=1).broadcast_to([P, E])
                         ).then_inc(late_in, 16)
            with sp.Fori(0, NPAIR // 2 - 1) as i:
                for par in range(2):
                    sp.wait_ge(wA_used, i * 2 + par + 1)
                    sp.dma_start(wA[par][:], w_attn[bass.ds(i * 2 + (par + 2), 1)].rearrange("o p n -> (o p) n")
                                 ).then_inc(wA_in[par], 16)
            with sp.Fori(0, NE // 2 - 1) as i:
                for par in range(2):
                    sp.wait_ge(down_ps, i * 2 + par + 1)
                    sp.dma_start(wE[par][:], w_exp[bass.ds(i * 2 + (par + 2), 1)].rearrange("o p n -> (o p) n")
                                 ).then_inc(wE_in[par], 16)
            sp.wait_ge(down_read, 2 * NE)
            sp.dma_start(out_dram, xs[:]).then_inc(out_done, 16)
            sp.wait_ge(out_done, 16)

        @block.gpsimd
        def _(pool):
            ch = Chain(pool, pool_chain)
            for m in (ident, identb):
                ch.step(nc.gpsimd.memset(m[:], 0.0))
                nc.gpsimd.affine_select(out=m[:], in_=m[:], compare_op=ALU.not_equal, fill=1.0, base=0,
                                        pattern=[[-1, P]], channel_multiplier=1).then_inc(ident_done, 1)
                pool.wait_ge(ident_done, 1 if m is ident else 2)
            for b in range(B):
                ch.step(nc.gpsimd.memset(V[b][:], 0.0))
                ch.step(nc.gpsimd.memset(V[b][:, :, XD:XD + 1], 1.0))
                ch.step(nc.gpsimd.memset(kparts[b][XK:XK + MR, :], 1.0))
            ch.step(nc.gpsimd.memset(one_row[:], 1.0))
            ch.step(nc.gpsimd.memset(cw[:, :, E:NE], 1.0))
            ch.step(nc.gpsimd.memset(qz[0][:], 0.0))
            nc.gpsimd.memset(qz[1][:], 0.0).then_inc(const_done, 1)

        @block.tensor
        def _(pe):
            mm, tr = nc.tensor.matmul, nc.tensor.transpose

            def norm_T(n):
                pe.wait_ge(ln_done, n)
                for k in range(KD):
                    for t in range(T):
                        last = tr(half[k][:, t * P:(t + 1) * P], xn[:, t, k * P:(k + 1) * P], ident[:])
                last.then_inc(xnT_ps, 1)

            def kv_proj(b, s):
                n = 2 * b + s
                kv, nat = half[2], half[3]
                pe.wait_ge(ctx_in[b][s], 16)
                if n == 0:
                    pe.wait_ge(wkv_in, 16)
                if n >= 1:
                    pe.wait_ge(kvT_done, n)
                for k in range(KD):
                    for j in range(4):
                        c = s * (S // 2) + j * 512
                        last = mm(kv[32 * j:32 * j + 32, :], wkv[:, k, :], ctx[b][:, k, c:c + 512],
                                  start=(k == 0), stop=(k == KD - 1))
                last.then_inc(kv_ps, 1)
                pe.wait_ge(kvT_done, n + 1)
                if n >= 1:
                    pe.wait_ge(kn_read, n)
                for t in range(4):
                    last = tr(nat[:, t * P:(t + 1) * P], kvT[:, n % 2, t * P:(t + 1) * P], ident[:])
                last.then_inc(kn_ps, 1)

            def k_T(b, s):
                n = 2 * b + s
                pe.wait_ge(k_asm, n + 1)
                for g in range(2):
                    if n >= 1:
                        pe.wait_ge(kt_done, 2 * n - 1 + g)
                    for j in range(8):
                        last = tr(half[g][:].bitcast(BF16)[0:XK, j * P:(j + 1) * P], kasm[:, 8 * g + j, :],
                                  identb[:])
                    last.then_inc(kt_ps, 1)

            def max_scores(w0, b, q0, n, k0):
                for j in range(n):
                    pe.wait_ge(xmax_read, w0 + (j - 1))
                    mm(XB[j % 2][:], qparts[0:XK, q0], kparts[b][0:XK, (k0 + j) * 512:(k0 + j + 1) * 512],
                       start=True, stop=True).then_inc(xmax_ready, 1)

            def max_rows(n):
                pe.wait_ge(mparts_ready, n + 1)
                if isinstance(n, int):
                    if n >= 2:
                        pe.wait_ge(accT_read, n - 1)
                else:
                    pe.wait_ge(accT_read, n - 1)
                for i in range(NBLK):
                    last = mm(MISC[XK:XK + MR, i * P:(i + 1) * P], mparts[:, i, :], identb[:],
                              start=True, stop=True)
                last.then_inc(mrows_ps, 1)

            def weighted(b, quad, n):
                pe.wait_ge(exp_done, n * 2 + 2)
                for j in range(4):
                    t = 4 * quad + j
                    last = mm(ACC[32 * j:32 * j + 32, :], V[b][:, t, :],
                              Pb[:, (2 * quad + j // 2) % 4, (j % 2) * 512:(j % 2) * 512 + 512],
                              start=(quad == 0), stop=(quad == QUADS - 1))
                last.then_inc(pv_done, 1)

            def chunk(b, c, g):
                cols = bass.ds(g * CW, CW)
                first = g if isinstance(g, int) else 1
                pe.wait_ge(mrows_ready, g + 1)
                for v in range(QUADS):
                    if v == QUADS - 1 and not (isinstance(g, int) and g == B * NCH - 1):
                        max_rows(g + 1)
                    for u in (2 * v, 2 * v + 1):
                        if not (isinstance(g, int) and g == 0 and u < 2):
                            pe.wait_ge(exp_done, g * 16 + (u - 1))
                        for j in range(2):
                            t = 2 * u + j
                            last = mm(pairS[u % 2][:, j * 512:(j + 1) * 512],
                                      kparts[b][:, t * P:(t + 1) * P], qparts[:, cols],
                                      start=True, stop=True)
                        last.then_inc(scores_ready, 1)
                    blk = g * NBLK + (AHEAD + v // 2)
                    nb = b + 1 if (c is not None and c * NBLK + AHEAD + v // 2 >= NCH * NBLK) else b
                    if nb < B:
                        max_scores(g * (NBLK * KC) + (AHEAD * KC + 4 * v), nb, bass.ds(blk * P, P), 4, 4 * (v % 2))
                    if v >= 1:
                        if v == 1 and not (isinstance(g, int) and g == 0):
                            pe.wait_ge(acc_saved, g)
                        weighted(b, v - 1, g * QUADS + (v - 1))
                    elif not (isinstance(g, int) and g == 0):
                        weighted(b if c != 0 else b - 1, QUADS - 1, g * QUADS - 1)
                    if v == 2 and not (isinstance(g, int) and g == 0):
                        sums_T(g - 1)

            def sums_T(g):
                pe.wait_ge(acc_saved, g + 1)
                if isinstance(g, int) and g == B * NCH - 1:
                    pe.wait_ge(accT_read, g)
                else:
                    pe.wait_ge(mrows_ready, g + 2)
                for i in range(NBLK):
                    last = tr(MISC[:, i * P:(i + 1) * P], accS[:, i * P:(i + 1) * P], ident[:])
                last.then_inc(accT_ps, 1)

            pe.wait_ge(ident_done, 2)
            norm_T(1)
            pe.wait_ge(xnT_done, 1)
            pe.wait_ge(wq_in, 16)
            for t in range(T):
                for k in range(KD):
                    last = mm(XB[t // 2][:, (t % 2) * D:(t % 2 + 1) * D], xnT[:, k, t * P:(t + 1) * P],
                              wq[:, k, :], start=(k == 0), stop=(k == KD - 1))
            last.then_inc(q_ps, 1)
            kv_proj(0, 0)
            for g in range(8):
                pe.wait_ge(q_asm, min(g + 1, 2))
                if g >= 2:
                    pe.wait_ge(qt_done, g - 1)
                for j in range(8):
                    last = tr(XB[g % 2][:].bitcast(BF16)[0:XK, j * P:(j + 1) * P],
                              qasm[:, 8 * g + j, :], identb[:])
                last.then_inc(qt_ps, 1)
            k_T(0, 0)
            kv_proj(0, 1)
            k_T(0, 1)
            pe.wait_ge(kt_done, 4)
            pe.wait_ge(qt_done, 8)
            for i in range(NBLK):
                for h in range(2):
                    w = KC * i + 4 * h
                    if w == 0:
                        for j in range(4):
                            if j >= 2:
                                pe.wait_ge(xmax_read, j - 1)
                            mm(XB[j % 2][:], qparts[0:XK, 0:P], kparts[0][0:XK, j * 512:(j + 1) * 512],
                               start=True, stop=True).then_inc(xmax_ready, 1)
                    else:
                        max_scores(w, 0, slice(i * P, (i + 1) * P), 4, 4 * h)
            for s in range(2):
                kv_proj(1, s)
                k_T(1, s)
            max_rows(0)
            max_scores(KC * NBLK, 0, slice(NBLK * P, AHEAD * P), KC, 0)
            pe.wait_ge(kt_done, 8)
            pe.wait_ge(const_done, 1)

            for b in range(B):
                chunk(b, 0, b * NCH)
                with pe.Fori(0, NCH - 3) as i:
                    chunk(b, None, i + (b * NCH + 1))
                chunk(b, NCH - 2, b * NCH + NCH - 2)
                chunk(b, NCH - 1, b * NCH + NCH - 1)
            G = B * NCH
            weighted(B - 1, QUADS - 1, G * QUADS - 1)
            sums_T(G - 1)

            pe.wait_ge(o_done, B * NCH)
            for k in range(KD):
                for t in range(T):
                    last = tr(half[k][:, t * P:(t + 1) * P], O[:, t, k * P:(k + 1) * P], ident[:])
            last.then_inc(oT_ps, 1)
            pe.wait_ge(oT_done, 1)
            pe.wait_ge(late_in, 16 * 5)
            for t in range(T):
                for k in range(KD):
                    last = mm(half[2 + t // 2][:, (t % 2) * D:(t % 2 + 1) * D], xnT[:, k, t * P:(t + 1) * P],
                              wcat[:, k, :], start=(k == 0), stop=(k == KD - 1))
            last.then_inc(y_ps, 1)

            norm_T(2)
            PJ, SB, PTB, AOB, OUTB = [half[0], half[1]], [half[2], half[3]], XB[0], XB[1], [ACC, MISC]
            pe.wait_ge(xnT_done, 2)

            def proj(p, par, turn, which):
                if which == 0:
                    pe.wait_ge(wA_in[par], turn * 16 + 16)
                if not (isinstance(p, int) and p == 0 and which < 2):
                    pe.wait_ge(proj_free[which], p + (1 if which == 2 else 0))
                for k in range(KD):
                    c = (k * 3 + which) * P
                    last = mm(PJ_of(par, which), wA[par][:, c:c + P], xnT[:, k, :], start=(k == 0), stop=(k == KD - 1))
                last.then_inc(proj_ps, 1)

            proj_free = {0: k_moved, 1: v_moved, 2: q_moved}

            def PJ_of(par, which):
                return PJ[(3 * par + which) % 2]

            def v_rows(p):
                pe.wait_ge(v_moved, p + 1)
                if not (isinstance(p, int) and p == 0):
                    pe.wait_ge(pT_done, p * 4)
                for t in range(T):
                    last = tr(PTB[:, t * P:(t + 1) * P], vTb[:, t * P:(t + 1) * P], ident[:])
                last.then_inc(vn_ps, 1)

            def attn_scores(p, par, u):
                b, h = u // 2, u % 2
                if u == 0:
                    pe.wait_ge(q_moved, p + 1)
                    pe.wait_ge(k_moved, p + 1)
                if not (isinstance(p, int) and p == 0 and u < 2):
                    pe.wait_ge(s_exp, p * 4 + (u - 1))
                for hf in range(2):
                    q0 = b * L + hf * P
                    last = mm(SB[u % 2][:, hf * L:(hf + 1) * L], qz[par][:, h, q0:q0 + P],
                              kTb[par][:, b * L:(b + 1) * L], start=True, stop=True)
                last.then_inc(s_ps, 1)

            def attn_values(p, par, u):
                b, h = u // 2, u % 2
                pe.wait_ge(s_norm, p * 4 + (u + 1))
                if u == 0:
                    pe.wait_ge(vn_done, p + 1)
                else:
                    pe.wait_ge(pT_done, p * 4 + u)
                for kt in range(2):
                    for hf in range(2):
                        last = tr(PTB[:, kt * L + hf * P:kt * L + (hf + 1) * P],
                                  sp_[:, u, hf * L + kt * P:hf * L + (kt + 1) * P], ident[:])
                last.then_inc(pT_ps, 1)

            def attn_out(p, par, u):
                b, h = u // 2, u % 2
                pe.wait_ge(pT_done, p * 4 + (u + 1))
                if u == 0 and not (isinstance(p, int) and p == 0):
                    pe.wait_ge(aT_done, p)
                for kt in range(2):
                    last = mm(AOB[64 * h:64 * h + 64, b * L:(b + 1) * L], vn[par][:, 2 * b + kt, 64 * h:64 * h + 64],
                              spT[:, u % 2, kt * L:(kt + 1) * L], start=(kt == 0), stop=(kt == 1))
                if u == 3:
                    last.then_inc(av_ps, 1)

            def pair(p, par, nxt):
                attn_scores(p, par, 0)
                attn_scores(p, par, 1)
                if nxt is not None:
                    proj(p + 1, 1 - par, nxt, 0)
                attn_values(p, par, 0)
                attn_scores(p, par, 2)
                attn_out(p, par, 0)
                if nxt is not None:
                    proj(p + 1, 1 - par, nxt, 1)
                attn_values(p, par, 1)
                attn_scores(p, par, 3)
                attn_out(p, par, 1)
                if nxt is not None:
                    proj(p + 1, 1 - par, nxt, 2)
                attn_values(p, par, 2)
                attn_out(p, par, 2)
                attn_values(p, par, 3)
                attn_out(p, par, 3)
                if nxt is not None:
                    v_rows(p + 1)
                pe.wait_ge(aT_done, p + 1)
                for t in range(T):
                    last = mm(OUTB[t // 2][:, (t % 2) * D:(t % 2 + 1) * D], aT[:, t * P:(t + 1) * P],
                              wA[par][:, KD * 3 * P:KD * 3 * P + D], start=False, stop=(False), skip_group_check=True)
                last.then_inc(wA_used, 1)

            for o in OUTB:
                mm(o[:], one_row[:], bo2[:].rearrange("o j n -> o (j n)"), start=True, stop=False,
                   skip_group_check=True)
            for w in range(3):
                proj(0, 0, 0, w)
            v_rows(0)
            pair(0, 0, 0)
            pair(1, 1, 1)
            with pe.Fori(1, NPAIR // 2 - 1) as i:
                pair(i * 2, 0, i)
                pair(i * 2 + 1, 1, i + 1)
            pair(NPAIR - 2, 0, NPAIR // 2 - 1)
            pair(NPAIR - 1, 1, None)

            norm_T(3)
            pe.wait_ge(xnT_done, 3)
            for t in range(T):
                for k in range(KD):
                    last = mm(MISC[:, t * E:(t + 1) * E], xnT[:, k, t * P:(t + 1) * P], gwT[:, k, :],
                              start=(k == 0), stop=(k == KD - 1))
            last.then_inc(gate_ps, 1)
            GB, UB, DB = [half[0], half[1]], [half[2], half[3]], [XB[0], XB[1]]

            def up(e, par, turn):
                pe.wait_ge(wE_in[par], turn * 16 + 16)
                if not (isinstance(e, int) and e < 2):
                    pe.wait_ge(hT_done, e - 1)
                for w, dst in ((0, GB), (1, UB)):
                    for k in range(KD):
                        c = (k * 2 + w) * P
                        last = mm(dst[par], wE[par][:, c:c + P], xnT[:, k, :], start=(k == 0), stop=(k == KD - 1))
                last.then_inc(up_ps, 1)

            def down(e, par):
                pe.wait_ge(hT_done, e + 1)
                for t in range(T):
                    if t % 2 == 0 and not (isinstance(e, int) and e == 0):
                        pe.wait_ge(down_read, e * 2 + (t // 2 - 1))
                    last = mm(DB[t // 2][:, (t % 2) * D:(t % 2 + 1) * D], hT[par][:, t * P:(t + 1) * P],
                              wE[par][:, KD * 2 * P:], start=True, stop=True)
                last.then_inc(down_ps, 1)

            up(0, 0, 0)
            up(1, 1, 0)
            down(0, 0)
            up(2, 0, 1)
            down(1, 1)
            with pe.Fori(1, NE // 2 - 1) as i:
                up(i * 2 + 1, 1, i)
                down(i * 2, 0)
                up(i * 2 + 2, 0, i + 1)
                down(i * 2 + 1, 1)
            up(NE - 1, 1, NE // 2 - 1)
            down(NE - 2, 0)
            down(NE - 1, 1)

        @block.scalar
        def _(act):
            A = nc.scalar.activation
            act.dma_start(wq[:], w_q.rearrange("(k p) n -> p k n", p=P)).then_inc(wq_in, 16)
            act.dma_start(wkv[:], w_kv.rearrange("(k p) n -> p k n", p=P)).then_inc(wkv_in, 16)

            def norm_move(n):
                act.wait_ge(xnT_ps, n)
                A(xnT[:].rearrange("p k n -> p (k n)"), pairS[0][:], ACT.Copy).then_inc(xnT_done, 1)

            def kv_move(b, s):
                n = 2 * b + s
                act.wait_ge(kv_ps, n + 1)
                if n >= 2:
                    act.wait_ge(kn_ps, n - 1)
                A(kvT[:, n % 2, :], half[2], ACT.Copy).then_inc(kvT_done, 1)

            def k_rows(b, s):
                n = 2 * b + s
                for g in range(2):
                    act.wait_ge(kt_ps, 2 * n + g + 1)
                    c = s * (S // 2) + g * 1024
                    A(kparts[b][0:XK, c:c + 1024], half[g].bitcast(BF16)[0:XK, :], ACT.Copy).then_inc(kt_done, 1)

            def max_move(n):
                act.wait_ge(mrows_ps, n + 1)
                A(qparts[XK:XK + MR, bass.ds(n * CW, CW)], MISC[XK:XK + MR, :], ACT.Copy).then_inc(mrows_ready, 1)

            def sums_move(g):
                act.wait_ge(pv_done, g * QUADS + QUADS)
                if not (isinstance(g, int) and g == 0):
                    act.wait_ge(accT_ps, g)
                A(accS[:], ACC[:], ACT.Copy).then_inc(acc_saved, 1)

            def chunk(c, g):
                zero = isinstance(g, int) and g == 0
                for u in range(KT // 2):
                    if u == 2 and not zero:
                        sums_move(g - 1)
                    if u == KT // 2 - 2 and not (isinstance(g, int) and g == B * NCH - 1):
                        max_move(g + 1)
                    act.wait_ge(scores_ready, g * 16 + (u + 1))
                    if u % 2 == 0 and not (zero and u < 4):
                        act.wait_ge(pv_done, g * QUADS + (u // 2 - 1))
                    A(Pb[:, u % 4, :], pairS[u % 2][:], ACT.Exp, scale=1.0 / np.sqrt(XD)).then_inc(exp_done, 1)

            norm_move(1)
            kv_move(0, 0)
            for g in range(8):
                if g % 2:
                    continue
                act.wait_ge(qt_ps, g + 1)
                if g:
                    act.wait_ge(qt_done, g)
                A(qparts[0:XK, g * 1024:(g + 1) * 1024], XB[g % 2][:].bitcast(BF16)[0:XK, :], ACT.Copy).then_inc(qt_done, 1)
            k_rows(0, 0)
            kv_move(0, 1)
            k_rows(0, 1)
            for s in range(2):
                kv_move(1, s)
                k_rows(1, s)
            max_move(0)
            for b in range(B):
                chunk(0, b * NCH)
                with act.Fori(0, NCH - 3) as i:
                    chunk(None, i + (b * NCH + 1))
                chunk(NCH - 2, b * NCH + NCH - 2)
                chunk(NCH - 1, b * NCH + NCH - 1)
            sums_move(B * NCH - 1)
            act.wait_ge(oT_ps, 1)
            A(xnT[:].rearrange("p k n -> p (k n)"), pairS[0][:], ACT.Copy).then_inc(oT_done, 1)
            norm_move(2)

            PJ, SB = [half[0], half[1]], [half[2], half[3]]

            def qkv_move(p, par):
                src = [PJ[(3 * par + w) % 2] for w in range(3)]
                bias = lambda w: wA[par][:, KD * 3 * P + D + w:KD * 3 * P + D + w + 1]
                return src, bias

            def q_move(p, par):
                src, bias = qkv_move(p, par)
                act.wait_ge(proj_ps, p * 3 + 1)
                if not (isinstance(p, int) and p < 2):
                    act.wait_ge(s_ps, p * 4 - 4)
                for h in range(2):
                    r = slice(64 * h, 64 * h + 64)
                    last = A(qz[par][r, h, :], src[0][r, :], ACT.Identity, bias=bias(0)[r, :])
                last.then_inc(q_moved, 1)

            def v_move(p, par):
                src, bias = qkv_move(p, par)
                act.wait_ge(proj_ps, p * 3 + 3)
                if not (isinstance(p, int) and p < 1):
                    act.wait_ge(vn_ps, p)
                A(vTb[:], src[2], ACT.Identity, bias=bias(2)).then_inc(v_moved, 1)

            def exps(p, u):
                act.wait_ge(s_max, p * 4 + (u + 1))
                if not (isinstance(p, int) and p == 0):
                    act.wait_ge(pT_ps, p * 4 + (u - 3))
                for hf in range(2):
                    last = A(sp_[:, u, hf * L:(hf + 1) * L], SB[u % 2][:, hf * L:(hf + 1) * L], ACT.Exp,
                             bias=snb[:, u, hf:hf + 1], scale=1.0 / np.sqrt(AD), accum_out=sden[:, u, hf:hf + 1])
                last.then_inc(s_exp, 1)

            def pair(p, par, nxt):
                exps(p, 0)
                exps(p, 1)
                if nxt is not None:
                    q_move(nxt, 1 - par)
                exps(p, 2)
                exps(p, 3)
                if nxt is not None:
                    v_move(nxt, 1 - par)
                act.wait_ge(av_ps, p + 1)
                if not (isinstance(p, int) and p == 0):
                    act.wait_ge(wA_used, p)
                A(aT, XB[1][:], ACT.Copy).then_inc(aT_done, 1)

            act.wait_ge(const_done, 1)
            q_move(0, 0)
            v_move(0, 0)
            pair(0, 0, 1)
            pair(1, 1, 2)
            with act.Fori(1, NPAIR // 2 - 1) as i:
                pair(i * 2, 0, i * 2 + 1)
                pair(i * 2 + 1, 1, i * 2 + 2)
            pair(NPAIR - 2, 0, NPAIR - 1)
            pair(NPAIR - 1, 1, None)

            norm_move(3)
            act.wait_ge(gate_ps, 1)
            A(Pb[:, 3, 0:T * E], MISC[:, 0:T * E], ACT.Exp, scale=-1.0).then_inc(gate_exp, 1)
            GB = [half[0], half[1]]

            def silu(e, par):
                act.wait_ge(up_ps, e + 1)
                if not (isinstance(e, int) and e < 2):
                    act.wait_ge(hT_done, e - 1)
                A(hsil[par], GB[par], ACT.Silu).then_inc(sil_done, 1)

            silu(0, 0)
            silu(1, 1)
            with act.Fori(1, NE // 2) as i:
                silu(i * 2, 0)
                silu(i * 2 + 1, 1)

        @block.vector
        def _(dve):
            ch = Chain(dve, dve_chain)
            TT, TS, CP = nc.vector.tensor_tensor, nc.vector.tensor_scalar, nc.vector.tensor_copy

            def layer_norm():
                for t in range(T):
                    ins = nc.vector.bn_stats(st6[:, t, :], xs[:, t, :])
                ch.step(ins)
                for t in range(T):
                    ins = nc.vector.bn_aggr(mv[:, t, :], st6[:, t, :])
                ch.step(ins)
                ch.step(TS(rv[:], mv[:, :, 1], EPS, None, ALU.add))
                ch.step(TS(ry[:].bitcast(I32), rv[:].bitcast(I32), -0.5, RSQRT_MAGIC, ALU.mult, ALU.add))
                for _ in range(4):
                    ch.step(TT(rt[:], ry[:], ry[:], ALU.mult))
                    ch.step(TT(rt[:], rt[:], rv[:], ALU.mult))
                    ch.step(TS(rt[:], rt[:], -0.5, 1.5, ALU.mult, ALU.add))
                    ch.step(TT(ry[:], ry[:], rt[:], ALU.mult))
                for t in range(T):
                    ins = TS(xn[:, t, :], xs[:, t, :], mv[:, t, 0:1], ry[:, t:t + 1], ALU.subtract, ALU.mult)
                ins.then_inc(ln_done, 1)

            def split(src, asm, n, part_of):
                first = [part_of.index(i) for i in (1, 2, 3)]
                grp = lambda i: asm[:, :, i * XD:(i + 1) * XD]
                r = res[:, 0:n * XD].rearrange("p (n d) -> p n d", d=XD)
                ch.step(CP(grp(first[0]), src))
                ch.step(TT(r, src, grp(first[0]), ALU.subtract))
                ch.step(CP(grp(first[1]), r))
                ins = TT(grp(first[2]), r, grp(first[1]), ALU.subtract)
                for i, part in enumerate(part_of):
                    if i not in first:
                        ins = CP(grp(i), grp(first[part - 1]))
                return ins

            def kv_rows(b, s):
                n = 2 * b + s
                dve.wait_ge(kn_ps, n + 1)
                if n:
                    dve.wait_ge(kt_ps, 2 * n)
                nat = half[3].rearrange("p (t j c) -> p j t c", t=4, j=4)
                tiles = V[b][:, s * 16:(s + 1) * 16, :].rearrange("p (j t) c -> p j t c", t=4)
                CP(tiles[:, :, :, 0:XD], nat[:, :, :, XD:2 * XD])
                ins = CP(kraw[:].rearrange("p (j t) c -> p j t c", t=4), nat[:, :, :, 0:XD])
                ins.then_inc(kn_read, 1)
                dve.wait_ge(kn_read, n + 1)
                split(kraw[:], kasm[:], KT // 2, K_PART).then_inc(k_asm, 1)

            def max_items(n, w0, slot, k0):
                for j in range(n):
                    dve.wait_ge(xmax_ready, w0 + (j + 1))
                    nc.vector.reduce_max(mxp[:, slot, k0 + j:k0 + j + 1], XB[j % 2][:], AX).then_inc(xmax_read, 1)

            def max_parts(n, w):
                dve.wait_ge(xmax_read, w)
                if not (isinstance(n, int) and n == 0):
                    dve.wait_ge(mrows_ps, n)
                ch.step(nc.vector.reduce_max(mres[:], mxp[:], AX))
                ch.step(TS(negm[:], mres[:], -1.0, None, ALU.mult))
                ch.step(CP(mparts[:, :, 0], negm[:]))
                ch.step(TT(mres[:], negm[:], mparts[:, :, 0], ALU.subtract))
                ch.step(CP(mparts[:, :, 1], mres[:]))
                TT(mparts[:, :, 2], mres[:], mparts[:, :, 1], ALU.subtract).then_inc(mparts_ready, 1)

            def sums_rows(b, c, g):
                dve.wait_ge(accT_ps, g + 1)
                if not (isinstance(g, int) and g == 0):
                    dve.wait_ge(o_done, g)
                ins = nc.vector.reduce_sum(osum[:], MISC[:].rearrange("p (i k c) -> p i c k", i=NBLK, k=4)[:, :, 0:XD + 1, :], AX)
                ins.then_inc(accT_read, 1)
                dve.wait_ge(accT_read, g + 1)
                ch.step(nc.vector.reciprocal(oden[:], osum[:, :, XD]))
                for i in range(NBLK):
                    ins = TS(O[:, 2 * b + i % 2, bass.ds(c * (2 * XD) + (i // 2) * XD, XD)], osum[:, i, 0:XD],
                             oden[:, i:i + 1], None, ALU.mult)
                ins.then_inc(o_done, 1)

            def chunk(b, c, g):
                for v in range(QUADS):
                    static = c is not None and isinstance(c, int)
                    nb = b + 1 if (static and c * NBLK + AHEAD + v // 2 >= NCH * NBLK) else b
                    if nb < B:
                        max_items(4, g * (NBLK * KC) + (AHEAD * KC + 4 * v), (AHEAD + v // 2) % NBLK, 4 * (v % 2))
                    if v == 3 and not (isinstance(g, int) and g == 0):
                        if static and c == 0:
                            sums_rows(b - 1, NCH - 1, g - 1)
                        else:
                            sums_rows(b, c - 1, g - 1)
                    if v == 5 and not (isinstance(g, int) and g == B * NCH - 1):
                        max_parts(g + 1, g * (NBLK * KC) + (AHEAD * KC + 24))

            dve.wait_ge(x_in, 16)
            layer_norm()
            dve.wait_ge(q_ps, 1)
            for b in range(B):
                src = XB[b][:].rearrange("p (t h d) -> p h t d", t=2, h=XH)
                ins = CP(Pb[:, b, 0:512].rearrange("p (h t d) -> p h t d", t=2, d=XD), src)
                ch.step(ins)
                split(Pb[:, b, 0:512].rearrange("p (n d) -> p n d", d=XD), qasm[:, 32 * b:32 * b + 32, :], 32,
                      Q_PART).then_inc(q_asm, 1)
            for g in range(1, 8, 2):
                dve.wait_ge(qt_ps, g + 1)
                dve.wait_ge(qt_done, g)
                CP(qparts[0:XK, g * 1024:(g + 1) * 1024], XB[g % 2][:].bitcast(BF16)[0:XK, :]).then_inc(qt_done, 1)
            dve.wait_ge(const_done, 1)
            kv_rows(0, 0)
            kv_rows(0, 1)
            for i in range(NBLK):
                max_items(KC, KC * i, i, 0)
            max_parts(0, KC * NBLK)
            kv_rows(1, 0)
            kv_rows(1, 1)
            max_items(KC, KC * NBLK, 0, 0)
            for b in range(B):
                chunk(b, 0, b * NCH)
                with dve.Fori(0, NCH - 3) as i:
                    ch.loop(i, 6)
                    chunk(b, i + 1, i + (b * NCH + 1))
                    ch.end(NCH - 3)
                chunk(b, NCH - 2, b * NCH + NCH - 2)
                chunk(b, NCH - 1, b * NCH + NCH - 1)
            sums_rows(B - 1, NCH - 1, B * NCH - 1)

            dve.wait_ge(y_ps, 1)
            for i in range(2):
                flat = xs[:].rearrange("p t d -> p (t d)")[:, i * 512:(i + 1) * 512]
                ins = TT(flat, half[2 + i], flat, ALU.add)
            ch.step(ins)
            layer_norm()

            PJ, SB = [half[0], half[1]], [half[2], half[3]]

            def k_move(p, par):
                dve.wait_ge(proj_ps, p * 3 + 2)
                if not (isinstance(p, int) and p < 2):
                    dve.wait_ge(s_ps, p * 4 - 4)
                c = KD * 3 * P + D + 1
                TS(kTb[par][:], PJ[(3 * par + 1) % 2], wA[par][:, c:c + 1], None, ALU.add).then_inc(k_moved, 1)

            def v_rows(p, par):
                dve.wait_ge(vn_ps, p + 1)
                if not (isinstance(p, int) and p < 2):
                    dve.wait_ge(av_ps, p - 1)
                CP(vn[par][:].rearrange("p t n -> p (t n)"), XB[0][:]).then_inc(vn_done, 1)

            def row_max(p, u):
                dve.wait_ge(s_ps, p * 4 + (u + 1))
                ch.step(nc.vector.reduce_max(smx[:, u, :], SB[u % 2].rearrange("p (h k) -> p h k", h=2), AX))
                TS(snb[:, u, :], smx[:, u, :], -1.0 / np.sqrt(AD), None, ALU.mult).then_inc(s_max, 1)

            def normalize(p, u):
                dve.wait_ge(s_exp, p * 4 + (u + 1))
                ch.step(nc.vector.reciprocal(srd[:, u, :], sden[:, u, :]))
                for hf in range(2):
                    w = sp_[:, u, hf * L:(hf + 1) * L]
                    ins = TS(w, w, srd[:, u, hf:hf + 1], None, ALU.mult)
                ins.then_inc(s_norm, 1)

            def pT_move(p, u):
                dve.wait_ge(pT_ps, p * 4 + (u + 1))
                CP(spT[:, u % 2, :], XB[0][:]).then_inc(pT_done, 1)

            def pair(p, par, nxt):
                row_max(p, 0)
                row_max(p, 1)
                normalize(p, 0)
                pT_move(p, 0)
                row_max(p, 2)
                normalize(p, 1)
                if nxt is not None:
                    k_move(nxt, 1 - par)
                pT_move(p, 1)
                row_max(p, 3)
                normalize(p, 2)
                pT_move(p, 2)
                normalize(p, 3)
                pT_move(p, 3)
                if nxt is not None:
                    v_rows(nxt, 1 - par)

            k_move(0, 0)
            v_rows(0, 0)
            pair(0, 0, 1)
            pair(1, 1, 2)
            with dve.Fori(0, NPAIR // 2 - 2) as i:
                ch.loop(i, 16)
                pair(i * 2 + 2, 0, i * 2 + 3)
                pair(i * 2 + 3, 1, i * 2 + 4)
                ch.end(NPAIR // 2 - 2)
            pair(NPAIR - 2, 0, NPAIR - 1)
            pair(NPAIR - 1, 1, None)
            dve.wait_ge(wA_used, NPAIR)
            for i, o in enumerate((ACC, MISC)):
                flat = xs[:].rearrange("p t d -> p (t d)")[:, i * 512:(i + 1) * 512]
                ins = TT(flat, o[:], flat, ALU.add)
            ch.step(ins)
            layer_norm()
            dve.wait_ge(ln_done, 3)
            ch.step(TT(xs[:], xs[:], xn[:], ALU.add))

            tmp = lambda i, n: Pb[:, 3, 64 + i:64 + i + n]
            sg = Pb[:, 3, 0:64]
            sfc = Pb[:, 3, 64:128]
            dve.wait_ge(gate_exp, 1)
            ch.step(TS(sg, sg, 1.0, None, ALU.add))
            ch.step(nc.vector.reciprocal(sg, sg))
            s3 = sg.rearrange("p (t e) -> p t e", t=T)
            c3 = sfc.rearrange("p (t e) -> p t e", t=T)
            ch.step(TT(c3, s3, gb[:].unsqueeze(1).broadcast_to([P, T, E]), ALU.add))
            c4 = sfc.rearrange("p (n a b) -> p n a b", a=2, b=2)
            hi = Pb[:, 3, 128:160].rearrange("p (n a) -> p n a", a=2)
            lo = Pb[:, 3, 160:192].rearrange("p (n a) -> p n a", a=2)
            TT(hi, c4[:, :, :, 0], c4[:, :, :, 1], ALU.max)
            ch.step(TT(lo, c4[:, :, :, 0], c4[:, :, :, 1], ALU.min))
            gs = Pb[:, 3, 192:208]
            g2 = Pb[:, 3, 208:240].rearrange("p (n a) -> p n a", a=2)
            TT(gs, hi[:, :, 0], hi[:, :, 1], ALU.add)
            ch.step(TT(g2, hi, lo, ALU.add))
            ch.step(TT(gs, gs, g2[:, :, 0], ALU.max))
            ch.step(TT(gs, gs, g2[:, :, 1], ALU.max))

            def ranks(vals, n, pair_cmp, rank):
                cmp4 = pair_cmp.rearrange("p (t i j) -> p t i j", t=T, i=n)
                for i in range(n):
                    me = vals[:, :, i:i + 1]
                    if i:
                        ins = TT(cmp4[:, :, i, 0:i], vals[:, :, 0:i], me.broadcast_to([P, T, i]), ALU.is_ge)
                    ins = TT(cmp4[:, :, i, i:n], vals[:, :, i:n], me.broadcast_to([P, T, n - i]), ALU.is_gt)
                ch.step(ins)
                ch.step(nc.vector.reduce_sum(rank, cmp4, AX))

            gr = Pb[:, 3, 240:256].rearrange("p (t g) -> p t g", t=T)
            ranks(gs.rearrange("p (t g) -> p t g", t=T), NG, Pb[:, 3, 256:320], gr)
            ch.step(TS(gr, gr, float(TG) - 0.5, None, ALU.is_lt))
            mk = Pb[:, 3, 320:384]
            mk4 = mk.rearrange("p (n e) -> p n e", e=E // NG)
            grb = Pb[:, 3, 240:256].unsqueeze(2).broadcast_to([P, T * NG, E // NG])
            ch.step(TT(mk4, sfc.rearrange("p (n e) -> p n e", e=E // NG), grb, ALU.mult))
            pen = Pb[:, 3, 384:400]
            ch.step(TS(pen, Pb[:, 3, 240:256], -1.0, BIG, ALU.add, ALU.mult))
            ch.step(TT(mk4, mk4, pen.unsqueeze(2).broadcast_to([P, T * NG, E // NG]), ALU.add))
            er = Pb[:, 3, 400:464].rearrange("p (t e) -> p t e", t=T)
            ranks(mk.rearrange("p (t e) -> p t e", t=T), E, Pb[:, 2, :], er)
            ch.step(TS(er, er, float(TOPK) - 0.5, None, ALU.is_lt))
            ch.step(TT(er, er, s3, ALU.mult))
            den = Pb[:, 3, 464:468]
            ch.step(nc.vector.reduce_sum(den, er, AX))
            ch.step(TS(den, den, 1e-20, None, ALU.add))
            ch.step(nc.vector.reciprocal(den, den))
            ch.step(TT(er, er, den.unsqueeze(2).broadcast_to([P, T, E]), ALU.mult))
            ch.step(TS(cw[:, :, 0:E], er, 2.5, None, ALU.mult))

            UB, DB = [half[2], half[3]], [XB[0], XB[1]]

            def hidden(e, par):
                dve.wait_ge(sil_done, e + 1)
                if not (isinstance(e, int) and e < 2):
                    dve.wait_ge(down_ps, e - 1)
                TT(hT[par], UB[par], hsil[par], ALU.mult).then_inc(hT_done, 1)

            def add_expert(e, cw_e):
                dve.wait_ge(down_ps, e + 1)
                for t in range(T):
                    ins = nc.vector.scalar_tensor_tensor(out=xs[:, t, :], in0=DB[t // 2][:, (t % 2) * D:(t % 2 + 1) * D],
                                                         scalar=cw[:, t, cw_e], in1=xs[:, t, :], op0=ALU.mult, op1=ALU.add)
                    if t % 2:
                        ins.then_inc(down_read, 1)
                return ins

            hidden(0, 0)
            hidden(1, 1)
            with dve.Fori(0, NE // 2 - 1) as i:
                dve.wait_ge(down_read, i * 4)
                add_expert(i * 2, bass.ds(i * 2, 1))
                hidden(i * 2 + 2, 0)
                dve.wait_ge(down_read, i * 4 + 2)
                add_expert(i * 2 + 1, bass.ds(i * 2 + 1, 1))
                hidden(i * 2 + 3, 1)
            dve.wait_ge(down_read, 2 * NE - 4)
            add_expert(NE - 2, slice(NE - 2, NE - 1))
            dve.wait_ge(down_read, 2 * NE - 2)
            add_expert(NE - 1, slice(NE - 1, NE))


def kernel(x, ctx_1024, L0_xattn_w_q, L0_xattn_w_kv, L0_xattn_w_concat, L0_attn_W_qkv, L0_attn_b_qkv, L0_attn_W_out,
           L0_attn_b_out, L0_ffn_gate_w, L0_ffn_gate_bias, L0_ffn_Wg, L0_ffn_Wu, L0_ffn_Wd, L0_ffn_Ws_g, L0_ffn_Ws_u,
           L0_ffn_Ws_d):
    import concourse.bacc as bacc
    from concourse.bass_utils import run_bass_kernel_spmd

    a = np.asarray
    wqkv = a(L0_attn_W_qkv).reshape(KD, P, 3, NPAIR, P).transpose(3, 1, 0, 2, 4).reshape(NPAIR, P, KD * 3 * P)
    wout = a(L0_attn_W_out).reshape(NPAIR, P, D)
    bqkv = a(L0_attn_b_qkv).reshape(3, NPAIR, P).transpose(1, 2, 0)
    w_attn = np.concatenate([wqkv, wout, bqkv], axis=2)

    def up(w):
        return a(w).reshape(-1, I, KD, P).transpose(0, 3, 2, 1)

    def pack(g, u, d):
        gu = np.stack([up(g), up(u)], axis=3).reshape(-1, P, KD * 2 * I)
        return np.concatenate([gu, d], axis=2)

    shared_d = a(L0_ffn_Ws_d).T.reshape(2, P, D)
    w_exp = np.concatenate([pack(L0_ffn_Wg, L0_ffn_Wu, a(L0_ffn_Wd).transpose(0, 2, 1)),
                            pack(L0_ffn_Ws_g, L0_ffn_Ws_u, shared_d)], axis=0)
    arrays = {
        "x": a(x),
        "ctxT": a(ctx_1024).transpose(0, 2, 1),
        "w_q": a(L0_xattn_w_q), "w_kv": a(L0_xattn_w_kv), "w_cat": a(L0_xattn_w_concat),
        "w_attn": w_attn, "b_out": a(L0_attn_b_out),
        "gate_wT": a(L0_ffn_gate_w).T, "gate_b": a(L0_ffn_gate_bias),
        "w_exp": w_exp,
    }
    arrays = {k: np.ascontiguousarray(v) for k, v in arrays.items()}
    nc = bacc.Bacc("TRN2", target_bir_lowering=False, num_devices=1)
    args = [nc.dram_tensor(k, v.shape, mybir.dt.from_np(v.dtype), kind="ExternalInput").ap()
            for k, v in arrays.items()]
    args.append(nc.dram_tensor("out", (B, L, D), F32, kind="ExternalOutput").ap())
    build(nc, *args)
    r = run_bass_kernel_spmd(nc, [arrays], core_ids=[0])
    return r.results[0]["out"]
```

```python
from contextlib import ExitStack

import numpy as np

import concourse.bass as bass
from concourse import mybir

ALU = mybir.AluOpType
ACT = mybir.ActivationFunctionType
AX = mybir.AxisListType.X
F32 = mybir.dt.float32
BF16 = mybir.dt.bfloat16
I32 = mybir.dt.int32

P = 128
B, L, D = 2, 256, 256
S = 4096
T = B * L // P
KD = D // P
XH, XD = 16, 16
NP6 = 6
XK = NP6 * XD
MR = 3
KT = S // P
CW = 512
NCH = XH * L // CW
NBLK = CW // P
KC = S // 512
AHEAD = NBLK + 1
QUADS = KT // 4
VW = 32
AH, AD = 16, 64
DIM = AH * AD
NPAIR = AH // 2
AQ = KD * 3 * P
E, I = 16, 128
NE = E + 2
EU = KD * 2 * P
NG, TG, TOPK = 4, 2, 4
EPS = 1e-5
RSQRT_MAGIC = float(0x5F3759DF)
BIG = 3.0e38

Q_PART = [1, 2, 1, 2, 3, 1]
K_PART = [1, 1, 2, 2, 1, 3]


class Chain:

    def __init__(self, eng, sem):
        self.eng, self.sem, self.n, self.extra = eng, sem, 0, 0

    def loop(self, turn, per):
        self.start, self.per, self.extra = self.n, per, turn * per

    def end(self, turns):
        assert self.n - self.start == self.per, (self.n - self.start, self.per)
        self.n += self.per * (turns - 1)
        self.extra = 0

    def step(self, ins):
        self.n += 1
        ins.then_inc(self.sem, 1)
        self.eng.wait_ge(self.sem, self.extra + self.n)


def build(nc, x, ctxT, w_q, w_kv, w_cat, w_qkv, b_qkv, w_out, b_out, gate_wT, gate_b, w_up, w_down, out):
    with ExitStack() as stack:
        def sb(name, shape, dt=F32):
            return stack.enter_context(nc.sbuf_tensor(name, shape, dt))

        def sem(name):
            return stack.enter_context(nc.semaphore(name))

        bank = [stack.enter_context(nc.psum_tensor(f"bank{i}", [P, 512], F32)) for i in range(4)]
        pairS = [stack.enter_context(nc.psum_tensor(f"pairS{i}", [P, 1024], F32)) for i in range(2)]
        XB = [bank[0], bank[1]]
        ACC = bank[2]
        MISC = bank[3]
        half = [pairS[0][:, 0:512], pairS[0][:, 512:1024], pairS[1][:, 0:512], pairS[1][:, 512:1024]]

        ident = sb("ident", [P, P])
        identb = sb("identb", [P, P], BF16)
        xs = sb("xs", [P, T, D])
        xn = sb("xn", [P, T, D])
        xnT = sb("xnT", [P, KD, B * L])
        st6 = sb("st6", [P, T, 6])
        mv = sb("mv", [P, T, 2])
        rv = sb("rv", [P, T])
        ry = sb("ry", [P, T])
        rt = sb("rt", [P, T])
        wq = sb("wq", [P, KD, D])
        wkv = sb("wkv", [P, KD, 2 * XD])
        wcat = sb("wcat", [P, KD, D])
        ctx = [sb(f"ctx{b}", [P, KD, S]) for b in range(B)]
        kvT = sb("kvT", [P, 2, 512])
        kraw = sb("kraw", [P, KT // 2, XD])
        res = sb("res", [P, 64 * XD])
        kasm = sb("kasm", [P, KT // 2, XK], BF16)
        qasm = sb("qasm", [P, 2 * XH * 2, XK], BF16)
        kparts = [sb(f"kparts{b}", [XK + MR, S], BF16) for b in range(B)]
        qparts = sb("qparts", [XK + MR, B * XH * L], BF16)
        V = [sb(f"V{b}", [P, KT, VW]) for b in range(B)]
        Pb = sb("Pb", [P, 4, 1024])
        mxp = sb("mxp", [P, NBLK, KC])
        negm = sb("negm", [P, NBLK])
        mres = sb("mres", [P, NBLK])
        mparts = sb("mparts", [P, NBLK, MR], BF16)
        accS = sb("accS", [P, 512])
        osum = sb("osum", [P, NBLK, XD + 1])
        oden = sb("oden", [P, NBLK])
        O = sb("O", [P, T, D])

        wA = [sb(f"wA{i}", [P, AQ]) for i in range(2)]
        wO = [sb(f"wO{i}", [P, D]) for i in range(2)]
        qz = [sb(f"qz{i}", [P, 2, B * L]) for i in range(2)]
        kTb = [sb(f"kTb{i}", [P, B * L]) for i in range(2)]
        vTb = sb("vTb", [P, B * L])
        vn = [sb(f"vn{i}", [P, T, P]) for i in range(2)]
        smx = sb("smx", [P, 4, 2])
        snb = sb("snb", [P, 4, 2])
        sden = sb("sden", [P, 4, 2])
        srd = sb("srd", [P, 4, 2])
        bqkv = sb("bqkv", [P, 3, NPAIR])
        bo2 = sb("bo2", [1, 2, D])
        one_row = sb("one_row", [1, P])
        wU = [sb(f"wU{i}", [P, EU]) for i in range(2)]
        wD = [sb(f"wD{i}", [P, D]) for i in range(2)]
        gwT = sb("gwT", [P, KD, E])
        gb = sb("gb", [P, E])
        cw = sb("cw", [P, T, NE])
        sp_ = Pb[:, 0:2, :].rearrange("p a (c k) -> p (a c) k", k=512)
        spT = Pb[:, 2, :].rearrange("p (a k) -> p a k", a=2)
        aT = [Pb[:, 3, 0:512], Pb[:, 3, 512:1024]]
        hsil = [Pb[:, 0, 0:512], Pb[:, 0, 512:1024]]
        hT = [Pb[:, 1, 0:512], Pb[:, 1, 512:1024]]

        x_in, wq_in, wkv_in = sem("x_in"), sem("wq_in"), sem("wkv_in")
        late_in = sem("late_in")
        ctx_in = [[sem(f"ctx_in{b}{s}") for s in range(2)] for b in range(B)]
        wA_in, wO_in, wU_in, wD_in = ([sem(f"{n}_in{i}") for i in range(2)] for n in ("wA", "wO", "wU", "wD"))
        out_done = sem("out_done")
        ident_done, const_done = sem("ident_done"), sem("const_done")
        dve_chain, act_chain, pool_chain = sem("dve_chain"), sem("act_chain"), sem("pool_chain")
        ln_done, xnT_ps, xnT_done = sem("ln_done"), sem("xnT_ps"), sem("xnT_done")
        q_ps, q_asm, qt_ps, qt_done = sem("q_ps"), sem("q_asm"), sem("qt_ps"), sem("qt_done")
        kv_ps, kvT_done, kn_ps, kn_read = sem("kv_ps"), sem("kvT_done"), sem("kn_ps"), sem("kn_read")
        k_asm, kt_ps, kt_done = sem("k_asm"), sem("kt_ps"), sem("kt_done")
        xmax_ready, xmax_read = sem("xmax_ready"), sem("xmax_read")
        mparts_ready, mrows_ps, mrows_ready = sem("mparts_ready"), sem("mrows_ps"), sem("mrows_ready")
        scores_ready, exp_done, pv_done = sem("scores_ready"), sem("exp_done"), sem("pv_done")
        acc_saved, accT_ps, accT_read = sem("acc_saved"), sem("accT_ps"), sem("accT_read")
        o_done, oT_ps, oT_done, y_ps = sem("o_done"), sem("oT_ps"), sem("oT_done"), sem("y_ps")
        proj_ps, q_moved, k_moved, v_moved = sem("proj_ps"), sem("q_moved"), sem("k_moved"), sem("v_moved")
        vn_ps, vn_done = sem("vn_ps"), sem("vn_done")
        s_ps, s_max, s_exp, s_norm = sem("s_ps"), sem("s_max"), sem("s_exp"), sem("s_norm")
        pT_ps, pT_done, av_ps, aT_done, ao_ps = sem("pT_ps"), sem("pT_done"), sem("av_ps"), sem("aT_done"), sem("ao_ps")
        wO_used = sem("wO_used")
        gate_ps, cw_done, gate_exp = sem("gate_ps"), sem("cw_done"), sem("gate_exp")
        up_ps, sil_done, hT_done, down_ps, down_read = (sem("up_ps"), sem("sil_done"), sem("hT_done"),
                                                        sem("down_ps"), sem("down_read"))

        x_dram = x.rearrange("b (t p) d -> p (b t) d", p=P)
        out_dram = out.rearrange("b (t p) d -> p (b t) d", p=P)

        block = stack.enter_context(nc.Block())

        @block.sync
        def _(sp):
            sp.dma_start(xs[:], x_dram).then_inc(x_in, 16)
            for b in range(B):
                for s in range(2):
                    c = slice(s * S // 2, (s + 1) * S // 2)
                    sp.dma_start(ctx[b][:, :, c], ctxT[b].rearrange("(k p) s -> p k s", p=P)[:, :, c]
                                 ).then_inc(ctx_in[b][s], 16)
            sp.dma_start(wcat[:], w_cat.rearrange("(k p) n -> p k n", p=P)).then_inc(late_in, 16)
            sp.dma_start(gwT[:], gate_wT.rearrange("(k p) n -> p k n", p=P)).then_inc(late_in, 16)
            def load(buf, src, n, landed):
                row = src[n] if isinstance(n, int) else src[bass.ds(n, 1)].rearrange("o p n -> (o p) n")
                sp.dma_start(buf[:], row).then_inc(landed, 16)

            for i in range(2):
                load(wA[i], w_qkv, i, wA_in[i])
                load(wO[i], w_out, i, wO_in[i])
            for i in range(2):
                load(wU[i], w_up, i, wU_in[i])
                load(wD[i], w_down, i, wD_in[i])
            sp.dma_start(bqkv[:], b_qkv).then_inc(late_in, 16)
            for j in range(2):
                sp.dma_start(bo2[:, j, :], b_out.rearrange("(o n) -> o n", o=1)).then_inc(late_in, 16)
            sp.dma_start(gb[:], gate_b.rearrange("(o n) -> o n", o=1).broadcast_to([P, E])
                         ).then_inc(late_in, 16)
            with sp.Fori(0, NPAIR // 2 - 1) as i:
                for par in range(2):
                    sp.wait_ge(proj_ps, i * 6 + (3 * par + 3))
                    load(wA[par], w_qkv, i * 2 + (par + 2), wA_in[par])
                    sp.wait_ge(wO_used, i * 2 + (par + 1))
                    load(wO[par], w_out, i * 2 + (par + 2), wO_in[par])
            with sp.Fori(0, NE // 2 - 1) as i:
                for par in range(2):
                    sp.wait_ge(up_ps, i * 2 + (par + 1))
                    load(wU[par], w_up, i * 2 + (par + 2), wU_in[par])
                    sp.wait_ge(down_ps, i * 2 + (par + 1))
                    load(wD[par], w_down, i * 2 + (par + 2), wD_in[par])
            sp.wait_ge(down_read, 2 * NE)
            sp.dma_start(out_dram, xs[:]).then_inc(out_done, 16)
            sp.wait_ge(out_done, 16)

        @block.gpsimd
        def _(pool):
            ch = Chain(pool, pool_chain)
            for m in (ident, identb):
                ch.step(nc.gpsimd.memset(m[:], 0.0))
                nc.gpsimd.affine_select(out=m[:], in_=m[:], compare_op=ALU.not_equal, fill=1.0, base=0,
                                        pattern=[[-1, P]], channel_multiplier=1).then_inc(ident_done, 1)
                pool.wait_ge(ident_done, 1 if m is ident else 2)
            for b in range(B):
                ch.step(nc.gpsimd.memset(V[b][:], 0.0))
                ch.step(nc.gpsimd.memset(V[b][:, :, XD:XD + 1], 1.0))
                ch.step(nc.gpsimd.memset(kparts[b][XK:XK + MR, :], 1.0))
            ch.step(nc.gpsimd.memset(one_row[:], 1.0))
            ch.step(nc.gpsimd.memset(cw[:, :, E:NE], 1.0))
            ch.step(nc.gpsimd.memset(qz[0][:], 0.0))
            nc.gpsimd.memset(qz[1][:], 0.0).then_inc(const_done, 1)

        @block.tensor
        def _(pe):
            mm, tr = nc.tensor.matmul, nc.tensor.transpose

            def norm_T(n):
                pe.wait_ge(ln_done, n)
                for k in range(KD):
                    for t in range(T):
                        last = tr(half[k][:, t * P:(t + 1) * P], xn[:, t, k * P:(k + 1) * P], ident[:])
                last.then_inc(xnT_ps, 1)

            def kv_proj(b, s):
                n = 2 * b + s
                kv, nat = half[2], half[3]
                pe.wait_ge(ctx_in[b][s], 16)
                if n == 0:
                    pe.wait_ge(wkv_in, 16)
                if n >= 1:
                    pe.wait_ge(kvT_done, n)
                for k in range(KD):
                    for j in range(4):
                        c = s * (S // 2) + j * 512
                        last = mm(kv[32 * j:32 * j + 32, :], wkv[:, k, :], ctx[b][:, k, c:c + 512],
                                  start=(k == 0), stop=(k == KD - 1))
                last.then_inc(kv_ps, 1)
                pe.wait_ge(kvT_done, n + 1)
                if n >= 1:
                    pe.wait_ge(kn_read, n)
                for t in range(4):
                    last = tr(nat[:, t * P:(t + 1) * P], kvT[:, n % 2, t * P:(t + 1) * P], ident[:])
                last.then_inc(kn_ps, 1)

            def k_T(b, s):
                n = 2 * b + s
                pe.wait_ge(k_asm, n + 1)
                for g in range(2):
                    if n >= 1:
                        pe.wait_ge(kt_done, 2 * n - 1 + g)
                    for j in range(8):
                        last = tr(half[g][:].bitcast(BF16)[0:XK, j * P:(j + 1) * P], kasm[:, 8 * g + j, :],
                                  identb[:])
                    last.then_inc(kt_ps, 1)

            def max_scores(w0, b, q0, n, k0):
                for j in range(n):
                    pe.wait_ge(xmax_read, w0 + (j - 1))
                    mm(XB[(k0 + j) % 2][:], qparts[0:XK, q0], kparts[b][0:XK, (k0 + j) * 512:(k0 + j + 1) * 512],
                       start=True, stop=True).then_inc(xmax_ready, 1)

            def max_rows(n):
                pe.wait_ge(mparts_ready, n + 1)
                if isinstance(n, int):
                    if n >= 2:
                        pe.wait_ge(accT_read, n - 1)
                else:
                    pe.wait_ge(accT_read, n - 1)
                for i in range(NBLK):
                    last = mm(MISC[XK:XK + MR, i * P:(i + 1) * P], mparts[:, i, :], identb[:],
                              start=True, stop=True)
                last.then_inc(mrows_ps, 1)

            def weighted(b, quad, n):
                pe.wait_ge(exp_done, n * 2 + 2)
                for j in range(4):
                    t = 4 * quad + j
                    last = mm(ACC[32 * j:32 * j + 32, :], V[b][:, t, :],
                              Pb[:, (2 * quad + j // 2) % 4, (j % 2) * 512:(j % 2) * 512 + 512],
                              start=(quad == 0), stop=(quad == QUADS - 1))
                last.then_inc(pv_done, 1)

            def chunk(b, c, g):
                cols = bass.ds(g * CW, CW)
                first = g if isinstance(g, int) else 1
                pe.wait_ge(mrows_ready, g + 1)
                for v in range(QUADS):
                    if v == QUADS - 1 and not (isinstance(g, int) and g == B * NCH - 1):
                        max_rows(g + 1)
                    blk = g * NBLK + (AHEAD + v // 2)
                    nb = b + 1 if (c is not None and c * NBLK + AHEAD + v // 2 >= NCH * NBLK) else b

                    def items(j, n):
                        if nb < B:
                            max_scores(g * (NBLK * KC) + (AHEAD * KC + 4 * v + j), nb, bass.ds(blk * P, P), n,
                                       4 * (v % 2) + j)

                    for u in (2 * v, 2 * v + 1):
                        items(u - 2 * v, 1)
                        if not (isinstance(g, int) and g == 0 and u < 2):
                            pe.wait_ge(exp_done, g * 16 + (u - 1))
                        for j in range(2):
                            t = 2 * u + j
                            last = mm(pairS[u % 2][:, j * 512:(j + 1) * 512],
                                      kparts[b][:, t * P:(t + 1) * P], qparts[:, cols],
                                      start=True, stop=True)
                        last.then_inc(scores_ready, 1)
                    items(2, 2)
                    if v >= 1:
                        if v == 1 and not (isinstance(g, int) and g == 0):
                            pe.wait_ge(acc_saved, g)
                        weighted(b, v - 1, g * QUADS + (v - 1))
                    elif not (isinstance(g, int) and g == 0):
                        weighted(b if c != 0 else b - 1, QUADS - 1, g * QUADS - 1)
                    if v == 2 and not (isinstance(g, int) and g == 0):
                        sums_T(g - 1)

            def sums_T(g):
                pe.wait_ge(acc_saved, g + 1)
                if isinstance(g, int) and g == B * NCH - 1:
                    pe.wait_ge(accT_read, g)
                else:
                    pe.wait_ge(mrows_ready, g + 2)
                for i in range(NBLK):
                    last = tr(MISC[:, i * P:(i + 1) * P], accS[:, i * P:(i + 1) * P], ident[:])
                last.then_inc(accT_ps, 1)

            pe.wait_ge(ident_done, 2)
            norm_T(1)
            pe.wait_ge(xnT_done, 1)
            pe.wait_ge(wq_in, 16)
            for t in range(T):
                for k in range(KD):
                    last = mm(XB[t // 2][:, (t % 2) * D:(t % 2 + 1) * D], xnT[:, k, t * P:(t + 1) * P],
                              wq[:, k, :], start=(k == 0), stop=(k == KD - 1))
            last.then_inc(q_ps, 1)
            kv_proj(0, 0)
            for g in range(8):
                pe.wait_ge(q_asm, min(g + 1, 2))
                if g >= 2:
                    pe.wait_ge(qt_done, g - 1)
                for j in range(8):
                    last = tr(XB[g % 2][:].bitcast(BF16)[0:XK, j * P:(j + 1) * P],
                              qasm[:, 8 * g + j, :], identb[:])
                last.then_inc(qt_ps, 1)
            k_T(0, 0)
            kv_proj(0, 1)
            k_T(0, 1)
            pe.wait_ge(kt_done, 4)
            pe.wait_ge(qt_done, 8)
            for i in range(NBLK):
                for h in range(2):
                    w = KC * i + 4 * h
                    if w == 0:
                        for j in range(4):
                            if j >= 2:
                                pe.wait_ge(xmax_read, j - 1)
                            mm(XB[j % 2][:], qparts[0:XK, 0:P], kparts[0][0:XK, j * 512:(j + 1) * 512],
                               start=True, stop=True).then_inc(xmax_ready, 1)
                    else:
                        max_scores(w, 0, slice(i * P, (i + 1) * P), 4, 4 * h)
            for s in range(2):
                kv_proj(1, s)
                k_T(1, s)
            max_rows(0)
            max_scores(KC * NBLK, 0, slice(NBLK * P, AHEAD * P), KC, 0)
            pe.wait_ge(kt_done, 8)
            pe.wait_ge(const_done, 1)

            for b in range(B):
                chunk(b, 0, b * NCH)
                with pe.Fori(0, NCH - 3) as i:
                    chunk(b, None, i + (b * NCH + 1))
                chunk(b, NCH - 2, b * NCH + NCH - 2)
                chunk(b, NCH - 1, b * NCH + NCH - 1)
            G = B * NCH
            weighted(B - 1, QUADS - 1, G * QUADS - 1)
            sums_T(G - 1)

            pe.wait_ge(o_done, B * NCH)
            for k in range(KD):
                for t in range(T):
                    last = tr(half[k][:, t * P:(t + 1) * P], O[:, t, k * P:(k + 1) * P], ident[:])
            last.then_inc(oT_ps, 1)
            pe.wait_ge(oT_done, 1)
            pe.wait_ge(late_in, 16 * 6)
            for t in range(T):
                for k in range(KD):
                    last = mm(half[2 + t // 2][:, (t % 2) * D:(t % 2 + 1) * D], xnT[:, k, t * P:(t + 1) * P],
                              wcat[:, k, :], start=(k == 0), stop=(k == KD - 1))
            last.then_inc(y_ps, 1)

            norm_T(2)
            PJ, SB, PTB, AOB, OUTB = [half[0], half[1]], [half[2], half[3]], XB[0], XB[1], [ACC, MISC]
            pe.wait_ge(xnT_done, 2)

            def proj(p, par, turn, which):
                if which == 0:
                    pe.wait_ge(wA_in[par], turn * 16 + 16)
                if not (isinstance(p, int) and p == 0 and which < 2):
                    pe.wait_ge(proj_free[which], p + (1 if which == 2 else 0))
                for k in range(KD):
                    c = (k * 3 + which) * P
                    last = mm(PJ_of(par, which), wA[par][:, c:c + P], xnT[:, k, :], start=(k == 0), stop=(k == KD - 1))
                last.then_inc(proj_ps, 1)

            proj_free = {0: k_moved, 1: vn_done, 2: q_moved}

            def PJ_of(par, which):
                return PJ[(3 * par + which) % 2]

            def v_rows(p, par):
                pe.wait_ge(v_moved, p + 1)
                for t in range(T):
                    last = tr(PJ_of(par, 2)[:, t * P:(t + 1) * P], vTb[:, t * P:(t + 1) * P], ident[:])
                last.then_inc(vn_ps, 1)

            def attn_scores(p, par, u):
                b, h = u // 2, u % 2
                if u == 0:
                    pe.wait_ge(q_moved, p + 1)
                    pe.wait_ge(k_moved, p + 1)
                if not (isinstance(p, int) and p == 0 and u < 2):
                    pe.wait_ge(s_exp, p * 4 + (u - 1))
                for hf in range(2):
                    q0 = b * L + hf * P
                    last = mm(SB[u % 2][:, hf * L:(hf + 1) * L], qz[par][:, h, q0:q0 + P],
                              kTb[par][:, b * L:(b + 1) * L], start=True, stop=True)
                last.then_inc(s_ps, 1)

            def attn_values(p, par, u):
                b, h = u // 2, u % 2
                pe.wait_ge(s_norm, p * 4 + (u + 1))
                if not (isinstance(p, int) and p == 0 and u == 0):
                    pe.wait_ge(pT_done, p * 4 + u)
                for kt in range(2):
                    for hf in range(2):
                        last = tr(PTB[:, kt * L + hf * P:kt * L + (hf + 1) * P],
                                  sp_[:, u, hf * L + kt * P:hf * L + (kt + 1) * P], ident[:])
                last.then_inc(pT_ps, 1)

            def attn_out(p, par, u):
                b, h = u // 2, u % 2
                pe.wait_ge(pT_done, p * 4 + (u + 1))
                if u == 0:
                    pe.wait_ge(vn_done, p + 1)
                    if not (isinstance(p, int) and p == 0):
                        pe.wait_ge(aT_done, p)
                for kt in range(2):
                    last = mm(AOB[64 * h:64 * h + 64, b * L:(b + 1) * L], vn[par][:, 2 * b + kt, 64 * h:64 * h + 64],
                              spT[:, u % 2, kt * L:(kt + 1) * L], start=(kt == 0), stop=(kt == 1))
                if u == 3:
                    last.then_inc(av_ps, 1)

            def out_product(p, par, turn):
                pe.wait_ge(aT_done, p + 1)
                pe.wait_ge(wO_in[par], turn * 16 + 16)
                for t in range(T):
                    last = mm(OUTB[t // 2][:, (t % 2) * D:(t % 2 + 1) * D], aT[par][:, t * P:(t + 1) * P],
                              wO[par][:], start=False, stop=False, skip_group_check=True)
                last.then_inc(wO_used, 1)

            def pair(p, par, nxt, before):
                attn_scores(p, par, 0)
                attn_scores(p, par, 1)
                if nxt is not None:
                    proj(p + 1, 1 - par, nxt, 0)
                attn_values(p, par, 0)
                attn_scores(p, par, 2)
                attn_out(p, par, 0)
                if nxt is not None:
                    proj(p + 1, 1 - par, nxt, 1)
                attn_values(p, par, 1)
                attn_scores(p, par, 3)
                attn_out(p, par, 1)
                if nxt is not None:
                    proj(p + 1, 1 - par, nxt, 2)
                attn_values(p, par, 2)
                if before is not None:
                    out_product(p - 1, 1 - par, before)
                attn_out(p, par, 2)
                attn_values(p, par, 3)
                if nxt is not None:
                    v_rows(p + 1, 1 - par)
                attn_out(p, par, 3)

            for o in OUTB:
                mm(o[:], one_row[:], bo2[:].rearrange("o j n -> o (j n)"), start=True, stop=False,
                   skip_group_check=True)
            for w in range(3):
                proj(0, 0, 0, w)
            v_rows(0, 0)
            pair(0, 0, 0, None)
            pair(1, 1, 1, 0)
            with pe.Fori(1, NPAIR // 2 - 1) as i:
                pair(i * 2, 0, i, i - 1)
                pair(i * 2 + 1, 1, i + 1, i)
            pair(NPAIR - 2, 0, NPAIR // 2 - 1, NPAIR // 2 - 2)
            pair(NPAIR - 1, 1, None, NPAIR // 2 - 1)
            out_product(NPAIR - 1, 1, NPAIR // 2 - 1)

            norm_T(3)
            pe.wait_ge(xnT_done, 3)
            for t in range(T):
                for k in range(KD):
                    last = mm(MISC[:, t * E:(t + 1) * E], xnT[:, k, t * P:(t + 1) * P], gwT[:, k, :],
                              start=(k == 0), stop=(k == KD - 1))
            last.then_inc(gate_ps, 1)
            GB, UB, DB = [half[0], half[1]], [half[2], half[3]], [XB[0], XB[1]]

            def up(e, par, turn):
                pe.wait_ge(wU_in[par], turn * 16 + 16)
                if not (isinstance(e, int) and e < 2):
                    pe.wait_ge(hT_done, e - 1)
                for w, dst in ((0, GB), (1, UB)):
                    for k in range(KD):
                        c = (k * 2 + w) * P
                        last = mm(dst[par], wU[par][:, c:c + P], xnT[:, k, :], start=(k == 0), stop=(k == KD - 1))
                last.then_inc(up_ps, 1)

            def down(e, par, turn):
                pe.wait_ge(wD_in[par], turn * 16 + 16)
                pe.wait_ge(hT_done, e + 1)
                for t in range(T):
                    if t % 2 == 0 and not (isinstance(e, int) and e == 0):
                        pe.wait_ge(down_read, e * 2 + (t // 2 - 1))
                    last = mm(DB[t // 2][:, (t % 2) * D:(t % 2 + 1) * D], hT[par][:, t * P:(t + 1) * P],
                              wD[par][:], start=True, stop=True)
                last.then_inc(down_ps, 1)

            up(0, 0, 0)
            up(1, 1, 0)
            down(0, 0, 0)
            up(2, 0, 1)
            down(1, 1, 0)
            with pe.Fori(1, NE // 2 - 1) as i:
                up(i * 2 + 1, 1, i)
                down(i * 2, 0, i)
                up(i * 2 + 2, 0, i + 1)
                down(i * 2 + 1, 1, i)
            up(NE - 1, 1, NE // 2 - 1)
            down(NE - 2, 0, NE // 2 - 1)
            down(NE - 1, 1, NE // 2 - 1)

        @block.scalar
        def _(act):
            A = nc.scalar.activation
            act.dma_start(wq[:], w_q.rearrange("(k p) n -> p k n", p=P)).then_inc(wq_in, 16)
            act.dma_start(wkv[:], w_kv.rearrange("(k p) n -> p k n", p=P)).then_inc(wkv_in, 16)

            def norm_move(n):
                act.wait_ge(xnT_ps, n)
                A(xnT[:].rearrange("p k n -> p (k n)"), pairS[0][:], ACT.Copy).then_inc(xnT_done, 1)

            def kv_move(b, s):
                n = 2 * b + s
                act.wait_ge(kv_ps, n + 1)
                if n >= 2:
                    act.wait_ge(kn_ps, n - 1)
                A(kvT[:, n % 2, :], half[2], ACT.Copy).then_inc(kvT_done, 1)

            def k_rows(b, s):
                n = 2 * b + s
                for g in range(2):
                    act.wait_ge(kt_ps, 2 * n + g + 1)
                    c = s * (S // 2) + g * 1024
                    A(kparts[b][0:XK, c:c + 1024], half[g].bitcast(BF16)[0:XK, :], ACT.Copy).then_inc(kt_done, 1)

            def max_move(n):
                act.wait_ge(mrows_ps, n + 1)
                A(qparts[XK:XK + MR, bass.ds(n * CW, CW)], MISC[XK:XK + MR, :], ACT.Copy).then_inc(mrows_ready, 1)

            def sums_move(g):
                act.wait_ge(pv_done, g * QUADS + QUADS)
                if not (isinstance(g, int) and g == 0):
                    act.wait_ge(accT_ps, g)
                A(accS[:], ACC[:], ACT.Copy).then_inc(acc_saved, 1)

            def chunk(c, g):
                zero = isinstance(g, int) and g == 0
                for u in range(KT // 2):
                    if u == 2 and not zero:
                        sums_move(g - 1)
                    if u == KT // 2 - 2 and not (isinstance(g, int) and g == B * NCH - 1):
                        max_move(g + 1)
                    act.wait_ge(scores_ready, g * 16 + (u + 1))
                    if u % 2 == 0 and not (zero and u < 4):
                        act.wait_ge(pv_done, g * QUADS + (u // 2 - 1))
                    A(Pb[:, u % 4, :], pairS[u % 2][:], ACT.Exp, scale=1.0 / np.sqrt(XD)).then_inc(exp_done, 1)

            norm_move(1)
            kv_move(0, 0)
            for g in range(8):
                if g % 2:
                    continue
                act.wait_ge(qt_ps, g + 1)
                if g:
                    act.wait_ge(qt_done, g)
                A(qparts[0:XK, g * 1024:(g + 1) * 1024], XB[g % 2][:].bitcast(BF16)[0:XK, :], ACT.Copy).then_inc(qt_done, 1)
            k_rows(0, 0)
            kv_move(0, 1)
            k_rows(0, 1)
            for s in range(2):
                kv_move(1, s)
                k_rows(1, s)
            max_move(0)
            for b in range(B):
                chunk(0, b * NCH)
                with act.Fori(0, NCH - 3) as i:
                    chunk(None, i + (b * NCH + 1))
                chunk(NCH - 2, b * NCH + NCH - 2)
                chunk(NCH - 1, b * NCH + NCH - 1)
            sums_move(B * NCH - 1)
            act.wait_ge(oT_ps, 1)
            A(xnT[:].rearrange("p k n -> p (k n)"), pairS[0][:], ACT.Copy).then_inc(oT_done, 1)
            norm_move(2)

            PJ, SB = [half[0], half[1]], [half[2], half[3]]

            def qkv_move(p, par):
                src = [PJ[(3 * par + w) % 2] for w in range(3)]
                bias = lambda w: bqkv[:, w, bass.ds(p, 1)]
                return src, bias

            def q_move(p, par):
                src, bias = qkv_move(p, par)
                act.wait_ge(proj_ps, p * 3 + 1)
                if not (isinstance(p, int) and p < 2):
                    act.wait_ge(s_ps, p * 4 - 4)
                for h in range(2):
                    r = slice(64 * h, 64 * h + 64)
                    last = A(qz[par][r, h, :], src[0][r, :], ACT.Identity, bias=bqkv[r, 0, bass.ds(p, 1)])
                last.then_inc(q_moved, 1)

            def v_move(p, par):
                src, bias = qkv_move(p, par)
                act.wait_ge(proj_ps, p * 3 + 3)
                if not (isinstance(p, int) and p < 1):
                    act.wait_ge(vn_ps, p)
                A(vTb[:], src[2], ACT.Identity, bias=bias(2)).then_inc(v_moved, 1)

            def exps(p, u):
                act.wait_ge(s_max, p * 4 + (u + 1))
                if not (isinstance(p, int) and p == 0):
                    act.wait_ge(pT_ps, p * 4 + (u - 3))
                for hf in range(2):
                    last = A(sp_[:, u, hf * L:(hf + 1) * L], SB[u % 2][:, hf * L:(hf + 1) * L], ACT.Exp,
                             bias=snb[:, u, hf:hf + 1], scale=1.0 / np.sqrt(AD), accum_out=sden[:, u, hf:hf + 1])
                last.then_inc(s_exp, 1)

            def pair(p, par, nxt):
                exps(p, 0)
                exps(p, 1)
                if nxt is not None:
                    q_move(p + 1, 1 - par)
                exps(p, 2)
                exps(p, 3)
                if nxt is not None:
                    v_move(p + 1, 1 - par)
                act.wait_ge(av_ps, p + 1)
                if not (isinstance(p, int) and p < 2):
                    act.wait_ge(wO_used, p - 1)
                A(aT[par], XB[1][:], ACT.Copy).then_inc(aT_done, 1)

            act.wait_ge(const_done, 1)
            act.wait_ge(late_in, 16 * 6)
            q_move(0, 0)
            v_move(0, 0)
            pair(0, 0, 0)
            pair(1, 1, 1)
            with act.Fori(1, NPAIR // 2 - 1) as i:
                pair(i * 2, 0, i)
                pair(i * 2 + 1, 1, i + 1)
            pair(NPAIR - 2, 0, NPAIR // 2 - 1)
            pair(NPAIR - 1, 1, None)

            norm_move(3)
            act.wait_ge(gate_ps, 1)
            A(Pb[:, 3, 0:T * E], MISC[:, 0:T * E], ACT.Exp, scale=-1.0).then_inc(gate_exp, 1)
            GB = [half[0], half[1]]

            def silu(e, par):
                act.wait_ge(up_ps, e + 1)
                if not (isinstance(e, int) and e < 2):
                    act.wait_ge(hT_done, e - 1)
                A(hsil[par], GB[par], ACT.Silu).then_inc(sil_done, 1)

            silu(0, 0)
            silu(1, 1)
            with act.Fori(1, NE // 2) as i:
                silu(i * 2, 0)
                silu(i * 2 + 1, 1)

        @block.vector
        def _(dve):
            ch = Chain(dve, dve_chain)
            TT, TS, CP = nc.vector.tensor_tensor, nc.vector.tensor_scalar, nc.vector.tensor_copy
            STT = nc.vector.scalar_tensor_tensor

            def layer_norm():
                for t in range(T):
                    ins = nc.vector.bn_stats(st6[:, t, :], xs[:, t, :])
                ch.step(ins)
                for t in range(T):
                    ins = nc.vector.bn_aggr(mv[:, t, :], st6[:, t, :])
                ch.step(ins)
                ch.step(TS(rv[:], mv[:, :, 1], EPS, None, ALU.add))
                ch.step(TS(ry[:].bitcast(I32), rv[:].bitcast(I32), -0.5, RSQRT_MAGIC, ALU.mult, ALU.add))
                for _ in range(3):
                    ch.step(TT(rt[:], ry[:], ry[:], ALU.mult))
                    ch.step(STT(out=rt[:], in0=rt[:], scalar=-0.5, in1=rv[:], op0=ALU.mult, op1=ALU.mult))
                    ch.step(STT(out=ry[:], in0=rt[:], scalar=1.5, in1=ry[:], op0=ALU.add, op1=ALU.mult))
                for t in range(T):
                    ins = TS(xn[:, t, :], xs[:, t, :], mv[:, t, 0:1], ry[:, t:t + 1], ALU.subtract, ALU.mult)
                ins.then_inc(ln_done, 1)

            def split(src, asm, n, part_of):
                first = [part_of.index(i) for i in (1, 2, 3)]
                grp = lambda i: asm[:, :, i * XD:(i + 1) * XD]
                r = res[:, 0:n * XD].rearrange("p (n d) -> p n d", d=XD)
                ch.step(CP(grp(first[0]), src))
                ch.step(TT(r, src, grp(first[0]), ALU.subtract))
                ch.step(CP(grp(first[1]), r))
                ins = TT(grp(first[2]), r, grp(first[1]), ALU.subtract)
                for i, part in enumerate(part_of):
                    if i not in first:
                        ins = CP(grp(i), grp(first[part - 1]))
                return ins

            def kv_rows(b, s):
                n = 2 * b + s
                dve.wait_ge(kn_ps, n + 1)
                if n:
                    dve.wait_ge(kt_ps, 2 * n)
                nat = half[3].rearrange("p (t j c) -> p j t c", t=4, j=4)
                tiles = V[b][:, s * 16:(s + 1) * 16, :].rearrange("p (j t) c -> p j t c", t=4)
                CP(tiles[:, :, :, 0:XD], nat[:, :, :, XD:2 * XD])
                ins = CP(kraw[:].rearrange("p (j t) c -> p j t c", t=4), nat[:, :, :, 0:XD])
                ins.then_inc(kn_read, 1)
                dve.wait_ge(kn_read, n + 1)
                split(kraw[:], kasm[:], KT // 2, K_PART).then_inc(k_asm, 1)

            def max_items(n, w0, slot, k0):
                for j in range(n):
                    dve.wait_ge(xmax_ready, w0 + (j + 1))
                    nc.vector.reduce_max(mxp[:, slot, k0 + j:k0 + j + 1], XB[j % 2][:], AX).then_inc(xmax_read, 1)

            def max_parts(n, w):
                dve.wait_ge(xmax_read, w)
                if not (isinstance(n, int) and n == 0):
                    dve.wait_ge(mrows_ps, n)
                ch.step(nc.vector.reduce_max(mres[:], mxp[:], AX))
                ch.step(TS(negm[:], mres[:], -1.0, None, ALU.mult))
                ch.step(CP(mparts[:, :, 0], negm[:]))
                ch.step(TT(mres[:], negm[:], mparts[:, :, 0], ALU.subtract))
                ch.step(CP(mparts[:, :, 1], mres[:]))
                TT(mparts[:, :, 2], mres[:], mparts[:, :, 1], ALU.subtract).then_inc(mparts_ready, 1)

            def sums_rows(b, c, g):
                dve.wait_ge(accT_ps, g + 1)
                if not (isinstance(g, int) and g == 0):
                    dve.wait_ge(o_done, g)
                ins = nc.vector.reduce_sum(osum[:], MISC[:].rearrange("p (i k c) -> p i c k", i=NBLK, k=4)[:, :, 0:XD + 1, :], AX)
                ins.then_inc(accT_read, 1)
                dve.wait_ge(accT_read, g + 1)
                ch.step(nc.vector.reciprocal(oden[:], osum[:, :, XD]))
                for i in range(NBLK):
                    ins = TS(O[:, 2 * b + i % 2, bass.ds(c * (2 * XD) + (i // 2) * XD, XD)], osum[:, i, 0:XD],
                             oden[:, i:i + 1], None, ALU.mult)
                ins.then_inc(o_done, 1)

            def chunk(b, c, g):
                for v in range(QUADS):
                    static = c is not None and isinstance(c, int)
                    nb = b + 1 if (static and c * NBLK + AHEAD + v // 2 >= NCH * NBLK) else b
                    if nb < B:
                        max_items(4, g * (NBLK * KC) + (AHEAD * KC + 4 * v), (AHEAD + v // 2) % NBLK, 4 * (v % 2))
                    if v == 3 and not (isinstance(g, int) and g == 0):
                        if static and c == 0:
                            sums_rows(b - 1, NCH - 1, g - 1)
                        else:
                            sums_rows(b, c - 1, g - 1)
                    if v == 5 and not (isinstance(g, int) and g == B * NCH - 1):
                        max_parts(g + 1, g * (NBLK * KC) + (AHEAD * KC + 24))

            dve.wait_ge(x_in, 16)
            layer_norm()
            dve.wait_ge(q_ps, 1)
            for b in range(B):
                src = XB[b][:].rearrange("p (t h d) -> p h t d", t=2, h=XH)
                ins = CP(Pb[:, b, 0:512].rearrange("p (h t d) -> p h t d", t=2, d=XD), src)
                ch.step(ins)
                split(Pb[:, b, 0:512].rearrange("p (n d) -> p n d", d=XD), qasm[:, 32 * b:32 * b + 32, :], 32,
                      Q_PART).then_inc(q_asm, 1)
            for g in range(1, 8, 2):
                dve.wait_ge(qt_ps, g + 1)
                dve.wait_ge(qt_done, g)
                CP(qparts[0:XK, g * 1024:(g + 1) * 1024], XB[g % 2][:].bitcast(BF16)[0:XK, :]).then_inc(qt_done, 1)
            dve.wait_ge(const_done, 1)
            kv_rows(0, 0)
            kv_rows(0, 1)
            for i in range(NBLK):
                max_items(KC, KC * i, i, 0)
            max_parts(0, KC * NBLK)
            kv_rows(1, 0)
            kv_rows(1, 1)
            max_items(KC, KC * NBLK, 0, 0)
            for b in range(B):
                chunk(b, 0, b * NCH)
                with dve.Fori(0, NCH - 3) as i:
                    ch.loop(i, 6)
                    chunk(b, i + 1, i + (b * NCH + 1))
                    ch.end(NCH - 3)
                chunk(b, NCH - 2, b * NCH + NCH - 2)
                chunk(b, NCH - 1, b * NCH + NCH - 1)
            sums_rows(B - 1, NCH - 1, B * NCH - 1)

            dve.wait_ge(y_ps, 1)
            for i in range(2):
                flat = xs[:].rearrange("p t d -> p (t d)")[:, i * 512:(i + 1) * 512]
                ins = TT(flat, half[2 + i], flat, ALU.add)
            ch.step(ins)
            layer_norm()

            PJ, SB = [half[0], half[1]], [half[2], half[3]]

            def k_move(p, par):
                dve.wait_ge(proj_ps, p * 3 + 2)
                if not (isinstance(p, int) and p < 2):
                    dve.wait_ge(s_ps, p * 4 - 4)
                TS(kTb[par][:], PJ[(3 * par + 1) % 2], bqkv[:, 1, bass.ds(p, 1)], None, ALU.add).then_inc(k_moved, 1)

            def v_rows(p, par):
                dve.wait_ge(vn_ps, p + 1)
                if not (isinstance(p, int) and p < 2):
                    dve.wait_ge(av_ps, p - 1)
                CP(vn[par][:].rearrange("p t n -> p (t n)"), PJ[(3 * par + 2) % 2]).then_inc(vn_done, 1)

            def row_max(p, u):
                dve.wait_ge(s_ps, p * 4 + (u + 1))
                ch.step(nc.vector.reduce_max(smx[:, u, :], SB[u % 2].rearrange("p (h k) -> p h k", h=2), AX))
                TS(snb[:, u, :], smx[:, u, :], -1.0 / np.sqrt(AD), None, ALU.mult).then_inc(s_max, 1)

            def normalize(p, u):
                dve.wait_ge(s_exp, p * 4 + (u + 1))
                ch.step(nc.vector.reciprocal(srd[:, u, :], sden[:, u, :]))
                for hf in range(2):
                    w = sp_[:, u, hf * L:(hf + 1) * L]
                    ins = TS(w, w, srd[:, u, hf:hf + 1], None, ALU.mult)
                ins.then_inc(s_norm, 1)

            def pT_move(p, u):
                dve.wait_ge(pT_ps, p * 4 + (u + 1))
                CP(spT[:, u % 2, :], XB[0][:]).then_inc(pT_done, 1)

            def pair(p, par, nxt):
                row_max(p, 0)
                row_max(p, 1)
                normalize(p, 0)
                pT_move(p, 0)
                row_max(p, 2)
                normalize(p, 1)
                if nxt is not None:
                    k_move(p + 1, 1 - par)
                pT_move(p, 1)
                row_max(p, 3)
                normalize(p, 2)
                pT_move(p, 2)
                normalize(p, 3)
                pT_move(p, 3)
                if nxt is not None:
                    v_rows(p + 1, 1 - par)

            dve.wait_ge(late_in, 16 * 6)
            k_move(0, 0)
            v_rows(0, 0)
            pair(0, 0, 0)
            pair(1, 1, 1)
            with dve.Fori(1, NPAIR // 2 - 1) as i:
                ch.loop(i - 1, 16)
                pair(i * 2, 0, i)
                pair(i * 2 + 1, 1, i + 1)
                ch.end(NPAIR // 2 - 2)
            pair(NPAIR - 2, 0, NPAIR // 2 - 1)
            pair(NPAIR - 1, 1, None)
            dve.wait_ge(wO_used, NPAIR)
            for i, o in enumerate((ACC, MISC)):
                flat = xs[:].rearrange("p t d -> p (t d)")[:, i * 512:(i + 1) * 512]
                ins = TT(flat, o[:], flat, ALU.add)
            ch.step(ins)
            layer_norm()
            dve.wait_ge(ln_done, 3)
            ch.step(TT(xs[:], xs[:], xn[:], ALU.add))

            tmp = lambda i, n: Pb[:, 3, 64 + i:64 + i + n]
            sg = Pb[:, 3, 0:64]
            sfc = Pb[:, 3, 64:128]
            dve.wait_ge(gate_exp, 1)
            ch.step(TS(sg, sg, 1.0, None, ALU.add))
            ch.step(nc.vector.reciprocal(sg, sg))
            s3 = sg.rearrange("p (t e) -> p t e", t=T)
            c3 = sfc.rearrange("p (t e) -> p t e", t=T)
            ch.step(TT(c3, s3, gb[:].unsqueeze(1).broadcast_to([P, T, E]), ALU.add))
            c4 = sfc.rearrange("p (n a b) -> p n a b", a=2, b=2)
            hi = Pb[:, 3, 128:160].rearrange("p (n a) -> p n a", a=2)
            lo = Pb[:, 3, 160:192].rearrange("p (n a) -> p n a", a=2)
            TT(hi, c4[:, :, :, 0], c4[:, :, :, 1], ALU.max)
            ch.step(TT(lo, c4[:, :, :, 0], c4[:, :, :, 1], ALU.min))
            gs = Pb[:, 3, 192:208]
            g2 = Pb[:, 3, 208:240].rearrange("p (n a) -> p n a", a=2)
            TT(gs, hi[:, :, 0], hi[:, :, 1], ALU.add)
            ch.step(TT(g2, hi, lo, ALU.add))
            ch.step(TT(gs, gs, g2[:, :, 0], ALU.max))
            ch.step(TT(gs, gs, g2[:, :, 1], ALU.max))

            def ranks(vals, n, pair_cmp, rank):
                cmp4 = pair_cmp.rearrange("p (t i j) -> p t i j", t=T, i=n)
                for i in range(n):
                    me = vals[:, :, i:i + 1]
                    if i:
                        ins = TT(cmp4[:, :, i, 0:i], vals[:, :, 0:i], me.broadcast_to([P, T, i]), ALU.is_ge)
                    ins = TT(cmp4[:, :, i, i:n], vals[:, :, i:n], me.broadcast_to([P, T, n - i]), ALU.is_gt)
                ch.step(ins)
                ch.step(nc.vector.reduce_sum(rank, cmp4, AX))

            gr = Pb[:, 3, 240:256].rearrange("p (t g) -> p t g", t=T)
            ranks(gs.rearrange("p (t g) -> p t g", t=T), NG, Pb[:, 3, 256:320], gr)
            ch.step(TS(gr, gr, float(TG) - 0.5, None, ALU.is_lt))
            mk = Pb[:, 3, 320:384]
            mk4 = mk.rearrange("p (n e) -> p n e", e=E // NG)
            grb = Pb[:, 3, 240:256].unsqueeze(2).broadcast_to([P, T * NG, E // NG])
            ch.step(TT(mk4, sfc.rearrange("p (n e) -> p n e", e=E // NG), grb, ALU.mult))
            pen = Pb[:, 3, 384:400]
            ch.step(TS(pen, Pb[:, 3, 240:256], -1.0, BIG, ALU.add, ALU.mult))
            ch.step(TT(mk4, mk4, pen.unsqueeze(2).broadcast_to([P, T * NG, E // NG]), ALU.add))
            er = Pb[:, 3, 400:464].rearrange("p (t e) -> p t e", t=T)
            ranks(mk.rearrange("p (t e) -> p t e", t=T), E, Pb[:, 2, :], er)
            ch.step(TS(er, er, float(TOPK) - 0.5, None, ALU.is_lt))
            ch.step(TT(er, er, s3, ALU.mult))
            den = Pb[:, 3, 464:468]
            ch.step(nc.vector.reduce_sum(den, er, AX))
            ch.step(TS(den, den, 1e-20, None, ALU.add))
            ch.step(nc.vector.reciprocal(den, den))
            ch.step(TT(er, er, den.unsqueeze(2).broadcast_to([P, T, E]), ALU.mult))
            ch.step(TS(cw[:, :, 0:E], er, 2.5, None, ALU.mult))

            UB, DB = [half[2], half[3]], [XB[0], XB[1]]

            def hidden(e, par):
                dve.wait_ge(sil_done, e + 1)
                if not (isinstance(e, int) and e < 2):
                    dve.wait_ge(down_ps, e - 1)
                TT(hT[par], UB[par], hsil[par], ALU.mult).then_inc(hT_done, 1)

            def add_expert(e, cw_e):
                dve.wait_ge(down_ps, e + 1)
                for t in range(T):
                    ins = nc.vector.scalar_tensor_tensor(out=xs[:, t, :], in0=DB[t // 2][:, (t % 2) * D:(t % 2 + 1) * D],
                                                         scalar=cw[:, t, cw_e], in1=xs[:, t, :], op0=ALU.mult, op1=ALU.add)
                    if t % 2:
                        ins.then_inc(down_read, 1)
                return ins

            hidden(0, 0)
            hidden(1, 1)
            add_expert(0, slice(0, 1))
            hidden(2, 0)
            dve.wait_ge(down_read, 2)
            add_expert(1, slice(1, 2))
            hidden(3, 1)
            with dve.Fori(1, NE // 2 - 1) as i:
                dve.wait_ge(down_read, i * 4)
                add_expert(i * 2, bass.ds(i * 2, 1))
                hidden(i * 2 + 2, 0)
                dve.wait_ge(down_read, i * 4 + 2)
                add_expert(i * 2 + 1, bass.ds(i * 2 + 1, 1))
                hidden(i * 2 + 3, 1)
            dve.wait_ge(down_read, 2 * NE - 4)
            add_expert(NE - 2, slice(NE - 2, NE - 1))
            dve.wait_ge(down_read, 2 * NE - 2)
            add_expert(NE - 1, slice(NE - 1, NE))


def kernel(x, ctx_1024, L0_xattn_w_q, L0_xattn_w_kv, L0_xattn_w_concat, L0_attn_W_qkv, L0_attn_b_qkv, L0_attn_W_out,
           L0_attn_b_out, L0_ffn_gate_w, L0_ffn_gate_bias, L0_ffn_Wg, L0_ffn_Wu, L0_ffn_Wd, L0_ffn_Ws_g, L0_ffn_Ws_u,
           L0_ffn_Ws_d):
    import concourse.bacc as bacc
    from concourse.bass_utils import run_bass_kernel_spmd

    a = np.asarray
    wqkv = a(L0_attn_W_qkv).reshape(KD, P, 3, NPAIR, P).transpose(3, 1, 0, 2, 4).reshape(NPAIR, P, KD * 3 * P)
    wout = a(L0_attn_W_out).reshape(NPAIR, P, D)
    bqkv = a(L0_attn_b_qkv).reshape(3, NPAIR, P).transpose(2, 0, 1)

    def up(w):
        return a(w).reshape(-1, I, KD, P).transpose(0, 3, 2, 1)

    def gate_up(g, u):
        return np.stack([up(g), up(u)], axis=3).reshape(-1, P, KD * 2 * I)

    shared_d = a(L0_ffn_Ws_d).T.reshape(2, P, D)
    w_up = np.concatenate([gate_up(L0_ffn_Wg, L0_ffn_Wu), gate_up(L0_ffn_Ws_g, L0_ffn_Ws_u)], axis=0)
    w_down = np.concatenate([a(L0_ffn_Wd).transpose(0, 2, 1), shared_d], axis=0)
    arrays = {
        "x": a(x),
        "ctxT": a(ctx_1024).transpose(0, 2, 1),
        "w_q": a(L0_xattn_w_q), "w_kv": a(L0_xattn_w_kv), "w_cat": a(L0_xattn_w_concat),
        "w_qkv": wqkv, "b_qkv": bqkv, "w_out": wout, "b_out": a(L0_attn_b_out),
        "gate_wT": a(L0_ffn_gate_w).T, "gate_b": a(L0_ffn_gate_bias),
        "w_up": w_up, "w_down": w_down,
    }
    arrays = {k: np.ascontiguousarray(v) for k, v in arrays.items()}
    nc = bacc.Bacc("TRN2", target_bir_lowering=False, num_devices=1)
    args = [nc.dram_tensor(k, v.shape, mybir.dt.from_np(v.dtype), kind="ExternalInput").ap()
            for k, v in arrays.items()]
    args.append(nc.dram_tensor("out", (B, L, D), F32, kind="ExternalOutput").ap())
    build(nc, *args)
    r = run_bass_kernel_spmd(nc, [arrays], core_ids=[0])
    return r.results[0]["out"]
```

```python
from contextlib import ExitStack

import numpy as np

import concourse.bass as bass
from concourse import mybir

ALU = mybir.AluOpType
ACT = mybir.ActivationFunctionType
AX = mybir.AxisListType.X
F32 = mybir.dt.float32
BF16 = mybir.dt.bfloat16
I32 = mybir.dt.int32
F32R = mybir.dt.float32r

P = 128
B, L, D = 2, 256, 256
S = 4096
T = B * L // P
KD = D // P
XH, XD = 16, 16
NP6 = 6
XK = NP6 * XD
MR = 3
KT = S // P
CW = 512
NCH = XH * L // CW
NBLK = CW // P
KC = S // 512
AHEAD = NBLK + 1
QUADS = KT // 4
VW = 32
AH, AD = 16, 64
DIM = AH * AD
NPAIR = AH // 2
AQ = KD * 3 * P
E, I = 16, 128
NE = 2 + E
EU = KD * 2 * P
NG, TG, TOPK = 4, 2, 4
EPS = 1e-5
RSQRT_MAGIC = float(0x5F3759DF)
BIG = 3.0e38
HIGH_BITS = -4096

Q_PART = [1, 2, 1, 2, 3, 1]
K_PART = [1, 1, 2, 2, 1, 3]


NITEM = NBLK * KC
ALL_ITEMS = B * NCH * NITEM


def ring_plan():
    turns = [*range(12), "sums", None, *range(12, 28), "rows", None, *range(28, NITEM)]
    assert len(turns) % 3 == 0
    plan = {}
    for n, use in enumerate(turns):
        back = n - 3
        while turns[back % len(turns)] is None:
            back -= 3
        plan[use] = (n % 3, turns[back % len(turns)], int(back < 0))
    return plan


PLAN = ring_plan()


def first_bank(w):
    return (w - AHEAD * KC) % 3


def first_item(w):
    return (w // 4 % NBLK, 4 * (w // 16) + w % 4) if w < NITEM else (NBLK, w - NITEM)


class Chain:

    def __init__(self, eng, sem):
        self.eng, self.sem, self.n, self.extra = eng, sem, 0, 0

    def loop(self, turn, per):
        self.start, self.per, self.extra = self.n, per, turn * per

    def end(self, turns):
        assert self.n - self.start == self.per, (self.n - self.start, self.per)
        self.n += self.per * (turns - 1)
        self.extra = 0

    def step(self, ins):
        self.n += 1
        ins.then_inc(self.sem, 1)
        self.eng.wait_ge(self.sem, self.extra + self.n)


def build(nc, x, ctxT, w_q, w_kv, w_cat, w_qkv, b_qkv, w_out, b_out, gate_wT, gate_b, w_up, w_down, out):
    with ExitStack() as stack:
        def sb(name, shape, dt=F32):
            return stack.enter_context(nc.sbuf_tensor(name, shape, dt))

        def sem(name):
            return stack.enter_context(nc.semaphore(name))

        bank = [stack.enter_context(nc.psum_tensor(f"bank{i}", [P, 512], F32)) for i in range(4)]
        pairS = [stack.enter_context(nc.psum_tensor(f"pairS{i}", [P, 1024], F32)) for i in range(2)]
        ACC = bank[2]
        MISC = bank[3]
        RING = [bank[0], bank[1], MISC]
        XB = [bank[0], bank[1]]
        half = [pairS[0][:, 0:512], pairS[0][:, 512:1024], pairS[1][:, 0:512], pairS[1][:, 512:1024]]

        ident = sb("ident", [P, P])
        identb = sb("identb", [P, P], BF16)
        xs = sb("xs", [P, T, D])
        xn = sb("xn", [P, T, D])
        xnT = sb("xnT", [P, KD, B * L])
        st6 = sb("st6", [P, T, 6])
        mv = sb("mv", [P, T, 2])
        rv = sb("rv", [P, T])
        ry = sb("ry", [P, T])
        rt = sb("rt", [P, T])
        wq = sb("wq", [P, KD, D])
        wkv = sb("wkv", [P, KD, 2 * XD])
        wcat = sb("wcat", [P, KD, D])
        ctx1 = sb("ctx1", [P, KD, S])
        kvT = sb("kvT", [P, 2, 512])
        kraw = sb("kraw", [P, 2, KT // 2, XD])
        resv = sb("resv", [P, 2 * XH * XD])
        resp = sb("resp", [P, 2 * XH * XD])
        kasm = sb("kasm", [P, 2, KT // 2, XK], BF16)
        qasm = sb("qasm", [P, 2 * XH * 2, XK], BF16)
        kparts = [sb(f"kparts{b}", [XK + MR, S], BF16) for b in range(B)]
        qparts = sb("qparts", [XK + MR, B * XH * L], BF16)
        V = [sb(f"V{b}", [P, KT, VW]) for b in range(B)]
        Pb = sb("Pb", [P, 4, 1024])
        mxp = sb("mxp", [P, NBLK, KC])
        mmax = sb("mmax", [P, NBLK])
        zero4 = sb("zero4", [P, NBLK])
        mparts = sb("mparts", [P, NBLK, MR], BF16)
        accS = sb("accS", [P, 512])
        osum = sb("osum", [P, NBLK, XD + 1])
        oden = sb("oden", [P, NBLK])
        O = sb("O", [P, T, D])

        wA = [sb(f"wA{i}", [P, AQ]) for i in range(2)]
        wO = [sb(f"wO{i}", [P, D]) for i in range(2)]
        qz = [sb(f"qz{i}", [P, 2, B * L]) for i in range(2)]
        kTb = [sb(f"kTb{i}", [P, B * L]) for i in range(2)]
        vTb = sb("vTb", [P, B * L])
        vn = [sb(f"vn{i}", [P, T, P]) for i in range(2)]
        smx = sb("smx", [P, 4, 2])
        snb = sb("snb", [P, 4, 2])
        sden = sb("sden", [P, 4, 2])
        srd = sb("srd", [P, 4, 2])
        bqkv = sb("bqkv", [P, 3, NPAIR])
        bo2 = sb("bo2", [1, 2, D])
        one_row = sb("one_row", [1, P])
        wU = [sb(f"wU{i}", [P, EU]) for i in range(2)]
        wD = [sb(f"wD{i}", [P, D]) for i in range(2)]
        gwT = sb("gwT", [P, KD, E])
        gb = sb("gb", [P, E])
        cw = sb("cw", [P, T, NE])
        qraw = Pb[:, 1, 0:512].rearrange("p (n d) -> p n d", d=XD)
        sp_ = Pb[:, 0:2, :].rearrange("p a (c k) -> p (a c) k", k=512)
        spT = Pb[:, 2, :].rearrange("p (a k) -> p a k", a=2)
        aT = [Pb[:, 3, 0:512], Pb[:, 3, 512:1024]]
        hsil = [Pb[:, 0, 0:512], Pb[:, 0, 512:1024]]
        hT = [Pb[:, 1, 0:512], Pb[:, 1, 512:1024]]

        with nc.sbuf_tensor("ctx0", [P, KD, S], F32) as ctx0:
            ctx = [ctx0, ctx1]
        xh, xl = sb("xh", [P, KD, B * L], F32R), sb("xl", [P, KD, B * L], F32R)
        wAh, wAl, wDh, wDl, hh, hl = ([sb(f"{name}{i}", [P, n], F32R) for i in range(2)] for name, n in (
            ("wAh", AQ), ("wAl", AQ), ("wDh", D), ("wDl", D), ("hh", 512), ("hl", 512)))
        wUh, wUl = [w[:, 0:EU] for w in wAh], [w[:, 0:EU] for w in wAl]
        spare = ctx1[:].rearrange("p k s -> p (k s)")
        room = lambda at, n: spare[:, at:at + n]
        xc = room(0, 1024).rearrange("p (k n) -> p k n", k=KD)
        wUc = [room(1024 + i * EU, EU) for i in range(2)]
        wDc = [room(2048 + i * D, D) for i in range(2)]
        hc = [room(2560 + i * 512, 512) for i in range(2)]
        wAc = [room(3584 + i * AQ, AQ) for i in range(2)]

        x_in, wq_in, wkv_in = sem("x_in"), sem("wq_in"), sem("wkv_in")
        late_in = sem("late_in")
        ctx_in = [[sem(f"ctx_in{b}{s}") for s in range(2)] for b in range(B)]
        wA_in, wO_in, wU_in, wD_in = ([sem(f"{n}_in{i}") for i in range(2)] for n in ("wA", "wO", "wU", "wD"))
        out_done = sem("out_done")
        v_init, qz_done = sem("v_init"), sem("qz_done")
        ident_done, const_done = sem("ident_done"), sem("const_done")
        dve_chain, act_chain, pool_chain = sem("dve_chain"), sem("act_chain"), sem("pool_chain")
        ln_done, xnT_ps, xnT_done = sem("ln_done"), sem("xnT_ps"), sem("xnT_done")
        q_ps, qraw_done, q_asm0, q_asm1 = sem("q_ps"), sem("qraw_done"), sem("q_asm0"), sem("q_asm1")
        q_split, k_split = sem("q_split"), sem("k_split")
        kv_ps, kvT_done, kn_ps, kn_read = sem("kv_ps"), sem("kvT_done"), sem("kn_ps"), sem("kn_read")
        k_asm, tp_ps, tp_done = sem("k_asm"), sem("tp_ps"), sem("tp_done")
        mmax_ready, osum_ready = sem("mmax_ready"), sem("osum_ready")
        xmax_ready, xmax_read = sem("xmax_ready"), sem("xmax_read")
        mparts_ready, mrows_ps, mrows_ready = sem("mparts_ready"), sem("mrows_ps"), sem("mrows_ready")
        scores_ready, exp_done, pv_done = sem("scores_ready"), sem("exp_done"), sem("pv_done")
        acc_saved, accT_ps, accT_read = sem("acc_saved"), sem("accT_ps"), sem("accT_read")
        o_done, oT_ps, oT_done, y_ps = sem("o_done"), sem("oT_ps"), sem("oT_done"), sem("y_ps")
        proj0_ps, q0_moved, k0_moved = sem("proj0_ps"), sem("q0_moved"), sem("k0_moved")
        proj_ps, q_moved, k_moved, v_moved = sem("proj_ps"), sem("q_moved"), sem("k_moved"), sem("v_moved")
        vn_ps, vn_done = sem("vn_ps"), sem("vn_done")
        s_ps, s_max, s_exp, s_norm = sem("s_ps"), sem("s_max"), sem("s_exp"), sem("s_norm")
        pT_ps, pT_done, av_ps, aT_done, ao_ps = sem("pT_ps"), sem("pT_done"), sem("av_ps"), sem("aT_done"), sem("ao_ps")
        wO_used = sem("wO_used")
        gate_ps, cw_done, gate_exp = sem("gate_ps"), sem("cw_done"), sem("gate_exp")
        x_cut, x_hi, x_lo = sem("x_cut"), sem("x_hi"), sem("x_lo")
        wA_cut, wA_hi, wA_lo = sem("wA_cut"), sem("wA_hi"), sem("wA_lo")
        wU_cut, wD_cut, hT_cut = sem("wU_cut"), sem("wD_cut"), sem("hT_cut")
        wU_hi, wU_lo, wD_hi, wD_lo, hT_hi, hT_lo = (sem(n) for n in ("wU_hi", "wU_lo", "wD_hi", "wD_lo",
                                                                     "hT_hi", "hT_lo"))
        up_ps, sil_done, hT_done, down_ps, down_read = (sem("up_ps"), sem("sil_done"), sem("hT_done"),
                                                        sem("down_ps"), sem("down_read"))

        GROUPS = ["q0", "k0", "k1", "q1", "q2", "k2", "k3", "q3", "q4", "q5", "q6", "q7", "k4", "k5", "k6", "k7"]

        def split(TT, CP, ch, src, asm, res, n, part_of, view=None):
            shape = view or (lambda ap: ap)
            first = [part_of.index(i) for i in (1, 2, 3)]
            grp = lambda i: asm[:, :, i * XD:(i + 1) * XD]
            r = res[:, 0:n * XD].rearrange("p (n d) -> p n d", d=XD)
            ch.step(CP(shape(grp(first[0])), src))
            ch.step(TT(shape(r), src, shape(grp(first[0])), ALU.subtract))
            ch.step(CP(grp(first[1]), r))
            return TT(grp(first[2]), r, grp(first[1]), ALU.subtract)

        def repeat(CP, asm, part_of):
            grp = lambda i: asm[:, :, i * XD:(i + 1) * XD]
            for i, part in enumerate(part_of):
                if i != part_of.index(part):
                    ins = CP(grp(i), grp(part_of.index(part)))
            return ins

        x_dram = x.rearrange("b (t p) d -> p (b t) d", p=P)
        out_dram = out.rearrange("b (t p) d -> p (b t) d", p=P)

        block = stack.enter_context(nc.Block())

        @block.sync
        def _(sp):
            sp.dma_start(xs[:], x_dram).then_inc(x_in, 16)
            sp.dma_start(wq[:], w_q.rearrange("(k p) n -> p k n", p=P)).then_inc(wq_in, 16)
            sp.dma_start(wkv[:], w_kv.rearrange("(k p) n -> p k n", p=P)).then_inc(wkv_in, 16)
            for b in range(B):
                for s in range(2):
                    c = slice(s * S // 2, (s + 1) * S // 2)
                    sp.dma_start(ctx[b][:, :, c], ctxT[b].rearrange("(k p) s -> p k s", p=P)[:, :, c]
                                 ).then_inc(ctx_in[b][s], 16)
            sp.dma_start(wcat[:], w_cat.rearrange("(k p) n -> p k n", p=P)).then_inc(late_in, 16)
            sp.dma_start(gwT[:], gate_wT.rearrange("(k p) n -> p k n", p=P)).then_inc(late_in, 16)
            def load(buf, src, n, landed):
                row = src[n] if isinstance(n, int) else src[bass.ds(n, 1)].rearrange("o p n -> (o p) n")
                sp.dma_start(buf[:], row).then_inc(landed, 16)

            for i in range(2):
                load(wA[i], w_qkv, i, wA_in[i])
                load(wO[i], w_out, i, wO_in[i])
            for i in range(2):
                load(wU[i], w_up, i, wU_in[i])
                load(wD[i], w_down, i, wD_in[i])
            sp.dma_start(bqkv[:], b_qkv).then_inc(late_in, 16)
            for j in range(2):
                sp.dma_start(bo2[:, j, :], b_out.rearrange("(o n) -> o n", o=1)).then_inc(late_in, 16)
            sp.dma_start(gb[:], gate_b.rearrange("(o n) -> o n", o=1).broadcast_to([P, E])
                         ).then_inc(late_in, 16)
            for n in (2, 3):
                sp.wait_ge(proj_ps, 3 * n - 3)
                load(wA[n % 2], w_qkv, n, wA_in[n % 2])
            with sp.Fori(0, NPAIR // 2 - 2) as i:
                for par in range(2):
                    sp.wait_ge(wO_used, i * 2 + (par + 1))
                    load(wO[par], w_out, i * 2 + (par + 2), wO_in[par])
                    sp.wait_ge(wA_lo, i * 2 + (par + 1))
                    load(wA[par], w_qkv, i * 2 + (par + 4), wA_in[par])
            for n in (NPAIR - 2, NPAIR - 1):
                sp.wait_ge(wO_used, n - 1)
                load(wO[n % 2], w_out, n, wO_in[n % 2])
            for n in (2, 3):
                sp.wait_ge(up_ps, n - 1)
                load(wU[n % 2], w_up, n, wU_in[n % 2])
            for n in (2, 3):
                sp.wait_ge(down_ps, n - 1)
                load(wD[n % 2], w_down, n, wD_in[n % 2])
                sp.wait_ge(wU_lo, n - 1)
                load(wU[n % 2], w_up, n + 2, wU_in[n % 2])
            with sp.Fori(0, NE // 2 - 3) as i:
                for par in range(2):
                    sp.wait_ge(wD_lo, i * 2 + (par + 1))
                    load(wD[par], w_down, i * 2 + (par + 4), wD_in[par])
                    sp.wait_ge(wU_lo, i * 2 + (par + 3))
                    load(wU[par], w_up, i * 2 + (par + 6), wU_in[par])
            for n in (NE - 2, NE - 1):
                sp.wait_ge(wD_lo, n - 3)
                load(wD[n % 2], w_down, n, wD_in[n % 2])
            for b in range(B):
                sp.wait_ge(down_read, 2 * NE - 1 + b)
                tiles = slice(2 * b, 2 * b + 2)
                sp.dma_start(out_dram[:, tiles, :], xs[:, tiles, :]).then_inc(out_done, 16)
            sp.wait_ge(out_done, 32)

        @block.gpsimd
        def _(pool):
            ch = Chain(pool, pool_chain)
            for m in (ident, identb):
                ch.step(nc.gpsimd.memset(m[:], 0.0))
                nc.gpsimd.affine_select(out=m[:], in_=m[:], compare_op=ALU.not_equal, fill=1.0, base=0,
                                        pattern=[[-1, P]], channel_multiplier=1).then_inc(ident_done, 1)
                pool.wait_ge(ident_done, 1 if m is ident else 2)
            ch.step(nc.gpsimd.memset(kparts[0][XK:XK + MR, :], 1.0))

            TT, CP = nc.gpsimd.tensor_tensor, nc.gpsimd.tensor_copy
            pool.wait_ge(qraw_done, 1)
            split(TT, CP, ch, qraw, qasm[:, 2 * XH:4 * XH, :], resp, 2 * XH, Q_PART).then_inc(q_split, 1)
            pool.wait_ge(q_split, 1)
            ch.step(nc.gpsimd.memset(kparts[1][XK:XK + MR, :], 1.0))
            ch.step(nc.gpsimd.memset(zero4[:], 0.0))
            ch.step(nc.gpsimd.memset(one_row[:], 1.0))
            nc.gpsimd.memset(cw[:, :, 0:2], 1.0).then_inc(const_done, 1)
            pool.wait_ge(const_done, 1)
            for n in (2, 3):
                pool.wait_ge(kn_read, n + 1)
                if n == 2:
                    pool.wait_ge(tp_ps, GROUPS.index("k1") + 1)
                else:
                    pool.wait_ge(tp_ps, GROUPS.index("k3") + 1)
                split(TT, CP, ch, kraw[:, n % 2], kasm[:, n % 2], resp, KT // 2, K_PART).then_inc(k_split, 1)
                pool.wait_ge(k_split, n - 1)

            def max_parts(n):
                pool.wait_ge(mmax_ready, n + 1)
                if not (isinstance(n, int) and n == 0):
                    pool.wait_ge(mrows_ps, n)
                ch.step(TT(mparts[:, :, 0], zero4[:], mmax[:], ALU.subtract))
                ch.step(TT(mmax[:], mmax[:], mparts[:, :, 0], ALU.add))
                ch.step(TT(mparts[:, :, 1], zero4[:], mmax[:], ALU.subtract))
                ch.step(TT(mmax[:], mmax[:], mparts[:, :, 1], ALU.add))
                TT(mparts[:, :, 2], zero4[:], mmax[:], ALU.subtract).then_inc(mparts_ready, 1)

            def divide(b, c, g):
                pool.wait_ge(osum_ready, g + 1)
                src = osum[:].rearrange("p (h t) c -> p h t c", t=2)
                den = oden[:].rearrange("p (h t o) -> p h t o", t=2, o=1)
                dst = O[:, 2 * b:2 * b + 2, bass.ds(c * (2 * XD), 2 * XD)].rearrange("p t (h d) -> p h t d", h=2)
                TT(dst, src[:, :, :, 0:XD], den.broadcast_to([P, 2, 2, XD]), ALU.mult
                   ).then_inc(o_done, 1)

            max_parts(0)
            for i in range(2):
                nc.gpsimd.memset(qz[i][:], 0.0).then_inc(qz_done, 1)
                pool.wait_ge(qz_done, i + 1)
            max_parts(1)
            for b in range(B):
                g = b * NCH
                if b:
                    divide(b - 1, NCH - 1, g - 1)
                    max_parts(g + 1)
                with pool.Fori(0, NCH - 3) as i:
                    ch.loop(i, 4)
                    divide(b, i, i + g)
                    max_parts(i + (g + 2))
                    ch.end(NCH - 3)
                for c in (NCH - 2, NCH - 1):
                    divide(b, c - 1, g + c - 1)
                    if g + c + 1 < B * NCH:
                        max_parts(g + c + 1)
            divide(B - 1, NCH - 1, B * NCH - 1)

            def low_x(n):
                pool.wait_ge(x_cut, n)
                TT(xl[:], xnT[:], xc, ALU.subtract).then_inc(x_lo, 1)
                pool.wait_ge(x_lo, n)

            def low_proj(p, par):
                pool.wait_ge(wA_cut, p - 1)
                pool.wait_ge(proj_ps, p * 3 - 3)
                TT(wAl[par][:], wA[par][:], wAc[par], ALU.subtract).then_inc(wA_lo, 1)
                pool.wait_ge(wA_lo, p - 1)

            pool.wait_ge(o_done, B * NCH)
            low_x(1)
            low_proj(2, 0)
            low_proj(3, 1)
            with pool.Fori(2, NPAIR // 2) as i:
                low_proj(i * 2, 0)
                low_proj(i * 2 + 1, 1)

            def low(dst, full, cut, e, cut_done, used, done):
                pool.wait_ge(cut_done, e - 1)
                if not (isinstance(e, int) and e < 4):
                    pool.wait_ge(used, e - 1)
                TT(dst, full, cut, ALU.subtract).then_inc(done, 1)
                pool.wait_ge(done, e - 1)

            def low_up(e, par):
                low(wUl[par], wU[par][:], wUc[par], e, wU_cut, up_ps, wU_lo)

            def low_down(e, par):
                low(wDl[par][:], wD[par][:], wDc[par], e, wD_cut, down_ps, wD_lo)

            def low_hidden(e, par):
                low(hl[par][:], hT[par], hc[par], e, hT_cut, down_ps, hT_lo)

            def low_turn(e):
                for par in range(2):
                    low_down(e + (2 + par), par)
                    low_hidden(e + (2 + par), par)
                    if not (isinstance(e, int) and e + 4 >= NE):
                        low_up(e + (4 + par), par)

            low_x(2)
            low_up(2, 0)
            low_up(3, 1)
            low_down(2, 0)
            low_hidden(2, 0)
            low_up(4, 0)
            low_down(3, 1)
            low_hidden(3, 1)
            low_up(5, 1)
            with pool.Fori(1, NE // 2 - 2) as i:
                low_turn(i * 2)
            low_turn(NE - 4)

        @block.tensor
        def _(pe):
            mm, tr = nc.tensor.matmul, nc.tensor.transpose

            def batch_T(src, b, dst):
                for k in range(KD):
                    for t in range(2):
                        last = tr(dst[:, k * L + t * P:k * L + (t + 1) * P],
                                  src[:, 2 * b + t, k * P:(k + 1) * P], ident[:])
                return last

            def norm_batch_T(n, b, dst):
                pe.wait_ge(ln_done, n)
                batch_T(xn, b, dst).then_inc(xnT_ps, 1)

            def kv_proj(b, s, parts=range(KD)):
                n = 2 * b + s
                kv, nat = half[2], half[3]
                if parts[0] == 0:
                    pe.wait_ge(ctx_in[b][s], 16)
                    if n == 0:
                        pe.wait_ge(wkv_in, 16)
                    if n >= 1:
                        pe.wait_ge(kvT_done, n)
                for k in parts:
                    for j in range(4):
                        c = s * (S // 2) + j * 512
                        last = mm(kv[32 * j:32 * j + 32, :], wkv[:, k, :], ctx[b][:, k, c:c + 512],
                                  start=(k == 0), stop=(k == KD - 1))
                if parts[-1] == KD - 1:
                    last.then_inc(kv_ps, 1)

            def kv_rows(b, s):
                n = 2 * b + s
                pe.wait_ge(kvT_done, n + 1)
                if n >= 1:
                    pe.wait_ge(kn_read, n)
                for t in range(4):
                    last = tr(half[3][:, t * P:(t + 1) * P], kvT[:, n % 2, t * P:(t + 1) * P], ident[:])
                last.then_inc(kn_ps, 1)

            def parts_T(name):
                n, m = GROUPS.index(name), int(name[1])
                if name[0] == "k":
                    pe.wait_ge(k_asm, m // 2 + 1)
                    src = lambda j: kasm[:, (m // 2) % 2, 8 * (m % 2) + j, :]
                else:
                    pe.wait_ge((q_asm0, q_asm1)[m // 4], 1)
                    src = lambda j: qasm[:, 8 * m + j, :]
                if n >= 2:
                    pe.wait_ge(tp_done, n - 1)
                for j in range(8):
                    last = tr(half[n % 2].bitcast(BF16)[0:XK, j * P:(j + 1) * P], src(j), identb[:])
                last.then_inc(tp_ps, 1)

            def first_items(w0, w1):
                for w in range(w0, w1):
                    if w >= 3:
                        pe.wait_ge(xmax_read, w - 2)
                    if w in (0, 2, 16, 18):
                        pe.wait_ge(tp_done, GROUPS.index({0: "k0", 2: "k1", 16: "k2", 18: "k3"}[w]) + 1)
                    blk, k = first_item(w)
                    mm(RING[first_bank(w)][:], qparts[0:XK, blk * P:(blk + 1) * P],
                       kparts[0][0:XK, k * 512:(k + 1) * 512], start=True, stop=True).then_inc(xmax_ready, 1)

            def ring_free(use, g):
                _, before, back = PLAN[use]
                n = g - back
                if before == "sums":
                    if not (isinstance(n, int) and n == 0):
                        pe.wait_ge(accT_read, n)
                elif before == "rows":
                    pe.wait_ge(mrows_ready, n + 2)
                else:
                    count = n * NITEM + (AHEAD * KC + before + 1)
                    pe.wait_ge(xmax_read, min(count, ALL_ITEMS) if isinstance(count, int) else count)

            def max_item(j, g, b, c):
                ahead = AHEAD + j // KC
                if c is not None and c * NBLK + ahead >= NCH * NBLK:
                    b = b + 1
                if b < B:
                    ring_free(j, g)
                    k = j % KC
                    mm(RING[PLAN[j][0]][:], qparts[0:XK, bass.ds(g * CW + ahead * P, P)],
                       kparts[b][0:XK, k * 512:(k + 1) * 512], start=True, stop=True).then_inc(xmax_ready, 1)

            def max_rows(n, dst):
                pe.wait_ge(mparts_ready, n + 1)
                for i in range(NBLK):
                    last = mm(dst[XK:XK + MR, i * P:(i + 1) * P], mparts[:, i, :], identb[:],
                              start=True, stop=True)
                last.then_inc(mrows_ps, 1)

            def weighted(b, quad, n):
                pe.wait_ge(exp_done, n * 2 + 2)
                for j in range(4):
                    t = 4 * quad + j
                    last = mm(ACC[32 * j:32 * j + 32, :], V[b][:, t, :],
                              Pb[:, (2 * quad + j // 2) % 4, (j % 2) * 512:(j % 2) * 512 + 512],
                              start=(quad == 0), stop=(quad == QUADS - 1))
                last.then_inc(pv_done, 1)

            def chunk(b, c, g):
                cols = bass.ds(g * CW, CW)
                pe.wait_ge(mrows_ready, g + 1)
                for v in range(QUADS):
                    if v == QUADS - 1 and not (isinstance(g, int) and g == B * NCH - 1):
                        ring_free("rows", g)
                        max_rows(g + 1, RING[PLAN["rows"][0]])
                    for u in (2 * v, 2 * v + 1):
                        max_item(2 * v + u, g, b, c)
                        if not (isinstance(g, int) and g == 0 and u < 2):
                            pe.wait_ge(exp_done, g * 16 + (u - 1))
                        for j in range(2):
                            t = 2 * u + j
                            last = mm(pairS[u % 2][:, j * 512:(j + 1) * 512],
                                      kparts[b][:, t * P:(t + 1) * P], qparts[:, cols],
                                      start=True, stop=True)
                        last.then_inc(scores_ready, 1)
                    max_item(4 * v + 2, g, b, c)
                    max_item(4 * v + 3, g, b, c)
                    if v >= 1:
                        if v == 1 and not (isinstance(g, int) and g == 0):
                            pe.wait_ge(acc_saved, g)
                        weighted(b, v - 1, g * QUADS + (v - 1))
                    elif not (isinstance(g, int) and g == 0):
                        weighted(b if c != 0 else b - 1, QUADS - 1, g * QUADS - 1)
                    if v == 2 and not (isinstance(g, int) and g == 0):
                        ring_free("sums", g)
                        sums_T(g - 1)
                    if isinstance(g, int) and g == B * NCH - 1:
                        if v == 2:
                            close_T(0)
                        if v == 3:
                            close_product(0)

            def close_T(b):
                pe.wait_ge(o_done, NCH * (b + 1))
                if b == 0:
                    pe.wait_ge(xmax_read, ALL_ITEMS)
                else:
                    pe.wait_ge(xnT_done, 3)
                batch_T(O, b, bank[1]).then_inc(oT_ps, 1)

            def close_product(b):
                if b == 0:
                    pe.wait_ge(late_in, 16 * 6)
                pe.wait_ge(oT_done, b + 1)
                for t in range(2):
                    for k in range(KD):
                        tok = b * L + t * P
                        last = mm(MISC[:, t * D:(t + 1) * D], xnT[:, k, tok:tok + P], wcat[:, k, :],
                                  start=(k == 0), stop=(k == KD - 1))
                last.then_inc(y_ps, 1)

            def sums_T(g):
                pe.wait_ge(acc_saved, g + 1)
                for i in range(NBLK):
                    last = tr(RING[PLAN["sums"][0]][:, i * P:(i + 1) * P], accS[:, i * P:(i + 1) * P], ident[:])
                last.then_inc(accT_ps, 1)

            pe.wait_ge(ident_done, 2)

            def q_proj(b, dst):
                pe.wait_ge(xnT_done, b + 1)
                if b == 0:
                    pe.wait_ge(wq_in, 16)
                for t in range(2):
                    for k in range(KD):
                        tok = (2 * b + t) * P
                        last = mm(dst[:, t * D:(t + 1) * D], xnT[:, k, tok:tok + P], wq[:, k, :],
                                  start=(k == 0), stop=(k == KD - 1))
                last.then_inc(q_ps, 1)

            norm_batch_T(1, 0, half[0])
            q_proj(0, ACC)
            norm_batch_T(2, 1, half[1])
            kv_proj(0, 0)
            q_proj(1, bank[0])
            kv_rows(0, 0)
            parts_T("q0")
            parts_T("k0")
            parts_T("k1")
            pe.wait_ge(qraw_done, 1)
            first_half, second_half = range(0, 1), range(1, KD)
            fill = {2: lambda: kv_proj(0, 1, first_half), 4: lambda: kv_proj(0, 1, second_half),
                    6: lambda: kv_rows(0, 1), 7: lambda: parts_T("q1"), 9: lambda: parts_T("q2"),
                    11: lambda: parts_T("k2"), 12: lambda: parts_T("k3"),
                    14: lambda: kv_proj(1, 0, first_half), 16: lambda: kv_proj(1, 0, second_half),
                    18: lambda: parts_T("q3"), 19: lambda: kv_rows(1, 0), 20: lambda: parts_T("q4"),
                    22: lambda: kv_proj(1, 1, first_half), 24: lambda: kv_proj(1, 1, second_half),
                    25: lambda: parts_T("q5"), 26: lambda: kv_rows(1, 1), 27: lambda: parts_T("q6"),
                    28: lambda: parts_T("q7"), 30: lambda: parts_T("k4"), 31: lambda: parts_T("k5"),
                    35: lambda: parts_T("k6"), 36: lambda: parts_T("k7")}
            for w in range(AHEAD * KC):
                if w in fill:
                    fill[w]()
                first_items(w, w + 1)
            max_rows(0, ACC)
            pe.wait_ge(tp_done, len(GROUPS))
            pe.wait_ge(const_done, 1)

            for b in range(B):
                chunk(b, 0, b * NCH)
                with pe.Fori(0, NCH - 3) as i:
                    chunk(b, None, i + (b * NCH + 1))
                chunk(b, NCH - 2, b * NCH + NCH - 2)
                chunk(b, NCH - 1, b * NCH + NCH - 1)
            G = B * NCH
            weighted(B - 1, QUADS - 1, G * QUADS - 1)
            norm_batch_T(3, 0, bank[1])
            pe.wait_ge(accT_read, G - 1)
            sums_T(G - 1)

            PJ, SB, PTB, AOB, OUTB = [half[0], half[1]], [half[2], half[3]], XB[0], XB[1], [ACC, MISC]

            def proj0(b, which):
                cols = slice(b * L, (b + 1) * L)
                for k in range(KD):
                    c = (k * 3 + which) * P
                    last = mm(PJ[which][:, cols], wA[0][:, c:c + P], xnT[:, k, cols],
                              start=(k == 0), stop=(k == KD - 1))
                last.then_inc(proj0_ps if b == 0 else proj_ps, 1)

            def proj(p, par, turn, which):
                halves = not (isinstance(p, int) and p < 2)
                if which == 0 and halves:
                    pe.wait_ge(wA_hi, p - 1)
                    pe.wait_ge(wA_lo, p - 1)
                    if isinstance(p, int) and p == 2:
                        pe.wait_ge(x_hi, 1)
                        pe.wait_ge(x_lo, 1)
                elif which == 0:
                    pe.wait_ge(wA_in[par], 16)
                pe.wait_ge(proj_free[which], p + (1 if which == 2 else 0))
                terms = ((wAh[par], xh), (wAh[par], xl), (wAl[par], xh)) if halves else ((wA[par], xnT),)
                for k in range(KD):
                    c = (k * 3 + which) * P
                    for n, (wt, xt) in enumerate(terms):
                        last = mm(PJ_of(par, which), wt[:, c:c + P], xt[:, k, :],
                                  start=(k == 0 and n == 0), stop=(k == KD - 1 and n == len(terms) - 1))
                last.then_inc(proj_ps, 1)

            proj_free = {0: k_moved, 1: vn_done, 2: q_moved}

            def PJ_of(par, which):
                return PJ[(3 * par + which) % 2]

            def v_rows(p, par):
                pe.wait_ge(v_moved, p + 1)
                for t in range(T):
                    last = tr(PJ_of(par, 2)[:, t * P:(t + 1) * P], vTb[:, t * P:(t + 1) * P], ident[:])
                last.then_inc(vn_ps, 1)

            def attn_scores(p, par, u):
                b, h = u // 2, u % 2
                if isinstance(p, int) and p == 0 and u == 0:
                    pe.wait_ge(q0_moved, 1)
                    pe.wait_ge(k0_moved, 1)
                elif u == (2 if isinstance(p, int) and p == 0 else 0):
                    pe.wait_ge(q_moved, p + 1)
                    pe.wait_ge(k_moved, p + 1)
                if not (isinstance(p, int) and p == 0 and u < 2):
                    pe.wait_ge(s_exp, p * 4 + (u - 1))
                for hf in range(2):
                    q0 = b * L + hf * P
                    last = mm(SB[u % 2][:, hf * L:(hf + 1) * L], qz[par][:, h, q0:q0 + P],
                              kTb[par][:, b * L:(b + 1) * L], start=True, stop=True)
                last.then_inc(s_ps, 1)

            def attn_values(p, par, u):
                b, h = u // 2, u % 2
                pe.wait_ge(s_norm, p * 4 + (u + 1))
                if not (isinstance(p, int) and p == 0 and u == 0):
                    pe.wait_ge(pT_done, p * 4 + u)
                for kt in range(2):
                    for hf in range(2):
                        last = tr(PTB[:, kt * L + hf * P:kt * L + (hf + 1) * P],
                                  sp_[:, u, hf * L + kt * P:hf * L + (kt + 1) * P], ident[:])
                last.then_inc(pT_ps, 1)

            def attn_out(p, par, u):
                b = u // 2
                pe.wait_ge(pT_done, p * 4 + (u + 2))
                if u == 0:
                    pe.wait_ge(vn_done, p + 1)
                    if not (isinstance(p, int) and p == 0):
                        pe.wait_ge(aT_done, p)
                for kt in range(2):
                    for h in range(2):
                        r = slice(64 * h, 64 * h + 64)
                        last = mm(AOB[r, b * L:(b + 1) * L], vn[par][:, 2 * b + kt, r],
                                  spT[:, h, kt * L:(kt + 1) * L], start=(kt == 0), stop=(kt == 1))
                last.then_inc(av_ps, 1)

            def out_product(p, par, turn, tiles=range(T)):
                pe.wait_ge(aT_done, p + (1 + tiles[0] // 2))
                pe.wait_ge(wO_in[par], turn * 16 + 16)
                for t in tiles:
                    last = mm(OUTB[t // 2][:, (t % 2) * D:(t % 2 + 1) * D], aT[par][:, t * P:(t + 1) * P],
                              wO[par][:], start=False, stop=False, skip_group_check=True)
                last.then_inc(wO_used, 1)

            def pair(p, par, nxt, before):
                for u in range(4):
                    attn_values(p, par, u)
                    if u < 2:
                        attn_scores(p, par, u + 2)
                    elif nxt is not None:
                        attn_scores(p + 1, 1 - par, u - 2)
                    if u < 3 and nxt is not None:
                        proj(p + 1, 1 - par, nxt, u)
                    if u == (3 if nxt is not None else 0) and before is not None:
                        out_product(p - 1, 1 - par, before)
                    if u == 3 and nxt is not None:
                        v_rows(p + 1, 1 - par)
                    if u % 2:
                        attn_out(p, par, u - 1)

            def begin_out(o):
                mm(o[:], one_row[:], bo2[:].rearrange("o j n -> o (j n)"), start=True, stop=False,
                   skip_group_check=True)

            pe.wait_ge(xnT_done, 3)
            pe.wait_ge(wA_in[0], 16)
            proj0(0, 0)
            proj0(0, 1)
            close_T(1)
            close_product(1)
            attn_scores(0, 0, 0)
            attn_scores(0, 0, 1)
            pe.wait_ge(acc_saved, G)
            begin_out(ACC)
            norm_batch_T(4, 1, bank[1])
            begin_out(MISC)
            pe.wait_ge(xnT_done, 4)
            proj0(1, 0)
            proj0(1, 1)
            proj(0, 0, 0, 2)
            v_rows(0, 0)
            pair(0, 0, 0, None)
            pair(1, 1, 1, 0)
            with pe.Fori(1, NPAIR // 2 - 1) as i:
                pair(i * 2, 0, i, i - 1)
                pair(i * 2 + 1, 1, i + 1, i)
            pair(NPAIR - 2, 0, NPAIR // 2 - 1, NPAIR // 2 - 2)
            q = NPAIR - 1
            attn_values(q, 1, 0)
            attn_scores(q, 1, 2)
            out_product(q - 1, 0, NPAIR // 2 - 1)
            attn_values(q, 1, 1)
            attn_scores(q, 1, 3)
            attn_out(q, 1, 0)
            attn_values(q, 1, 2)
            out_product(q, 1, NPAIR // 2 - 1, range(0, 2))
            attn_values(q, 1, 3)
            attn_out(q, 1, 2)
            out_product(q, 1, NPAIR // 2 - 1, range(2, 4))

            GB, UB, DB = [half[0], half[1]], [half[2], half[3]], [XB, [ACC, MISC]]

            def gate(b):
                for t in (2 * b, 2 * b + 1):
                    for k in range(KD):
                        last = mm(ACC[:, t * E:(t + 1) * E], xnT[:, k, t * P:(t + 1) * P], gwT[:, k, :],
                                  start=(k == 0), stop=(k == KD - 1))
                return last

            def up_batch(e, b):
                cols = slice(b * L, (b + 1) * L)
                if b == 0:
                    pe.wait_ge(wU_in[e], 16)
                for w, dst in ((0, GB), (1, UB)):
                    for k in range(KD):
                        c = (k * 2 + w) * P
                        last = mm(dst[e][:, cols], wU[e][:, c:c + P], xnT[:, k, cols],
                                  start=(k == 0), stop=(k == KD - 1))
                if b == 1:
                    last.then_inc(up_ps, 1)

            def up(e, par):
                pe.wait_ge(wU_hi, e - 1)
                pe.wait_ge(wU_lo, e - 1)
                pe.wait_ge(hT_done, e - 1)
                for w, dst in ((0, GB), (1, UB)):
                    for n, (wt, xt, k) in enumerate((wt, xt, k) for k in range(KD)
                                                    for wt, xt in ((wUh[par], xh), (wUh[par], xl), (wUl[par], xh))):
                        c = (k * 2 + w) * P
                        last = mm(dst[par], wt[:, c:c + P], xt[:, k, :],
                                  start=(n == 0), stop=(n == 3 * KD - 1))
                last.then_inc(up_ps, 1)

            def down(e, par):
                if isinstance(e, int) and e < 2:
                    pe.wait_ge(wD_in[par], 16)
                    pe.wait_ge(hT_done, e + 1)
                    terms = ((hT[par], wD[par][:]),)
                else:
                    for both_halves in (wD_hi, wD_lo, hT_hi, hT_lo):
                        pe.wait_ge(both_halves, e - 1)
                    terms = ((hh[par], wDh[par][:]), (hh[par], wDl[par][:]), (hl[par], wDh[par][:]))
                for t in range(T):
                    if t % 2 == 0 and not (isinstance(e, int) and e < 2):
                        pe.wait_ge(down_read, e * 2 + (t // 2 - 3))
                    for n, (ht, wt) in enumerate(terms):
                        last = mm(DB[par][t // 2][:, (t % 2) * D:(t % 2 + 1) * D],
                                  ht[:, t * P:(t + 1) * P], wt,
                                  start=(n == 0), stop=(n == len(terms) - 1))
                last.then_inc(down_ps, 1)

            norm_batch_T(5, 0, XB[0])
            pe.wait_ge(xnT_done, 5)
            up_batch(0, 0)
            gate(0)
            up_batch(1, 0)
            norm_batch_T(6, 1, XB[1])
            pe.wait_ge(xnT_done, 6)
            up_batch(0, 1)
            gate(1).then_inc(gate_ps, 1)
            up_batch(1, 1)
            down(0, 0)
            pe.wait_ge(x_hi, 2)
            pe.wait_ge(x_lo, 2)
            up(2, 0)
            down(1, 1)
            with pe.Fori(1, NE // 2 - 1) as i:
                up(i * 2 + 1, 1)
                down(i * 2, 0)
                up(i * 2 + 2, 0)
                down(i * 2 + 1, 1)
            up(NE - 1, 1)
            down(NE - 2, 0)
            down(NE - 1, 1)

        @block.scalar
        def _(act):
            A = nc.scalar.activation

            def batch_move(b, src):
                return A(xnT[:, :, b * L:(b + 1) * L], src.rearrange("p (k n) -> p k n", k=KD), ACT.Copy)

            def norm_batch_move(n, b, src):
                act.wait_ge(xnT_ps, n)
                batch_move(b, src).then_inc(xnT_done, 1)

            def close_move(b):
                act.wait_ge(oT_ps, b + 1)
                batch_move(b, bank[1][:]).then_inc(oT_done, 1)

            def kv_move(b, s):
                n = 2 * b + s
                act.wait_ge(kv_ps, n + 1)
                if n >= 2:
                    act.wait_ge(kn_ps, n - 1)
                A(kvT[:, n % 2, :], half[2], ACT.Copy).then_inc(kvT_done, 1)

            def kv_rows(b, s):
                n = 2 * b + s
                act.wait_ge(kn_ps, n + 1)
                if n == 2:
                    act.wait_ge(k_asm, 1)
                else:
                    act.wait_ge(k_asm, 2)
                nat = half[3].rearrange("p (t j c) -> p j t c", t=4, j=4)
                A(V[b][:, s * 16:(s + 1) * 16, 0:XD].rearrange("p (j t) c -> p j t c", t=4),
                  nat[:, :, :, XD:2 * XD], ACT.Copy)
                A(kraw[:, n % 2].rearrange("p (j t) c -> p j t c", t=4), nat[:, :, :, 0:XD], ACT.Copy).then_inc(kn_read, 1)

            def parts_move(*names):
                for name in names:
                    n, m = GROUPS.index(name), int(name[1])
                    act.wait_ge(tp_ps, n + 1)
                    dst = kparts[m // 4][0:XK, (m % 4) * 1024:(m % 4 + 1) * 1024] if name[0] == "k" else \
                        qparts[0:XK, m * 1024:(m + 1) * 1024]
                    A(dst, half[n % 2].bitcast(BF16)[0:XK, :], ACT.Copy).then_inc(tp_done, 1)

            def max_move(n, src):
                act.wait_ge(mrows_ps, n + 1)
                A(qparts[XK:XK + MR, bass.ds(n * CW, CW)], src[XK:XK + MR, :], ACT.Copy).then_inc(mrows_ready, 1)

            def sums_move(g):
                act.wait_ge(pv_done, g * QUADS + QUADS)
                if not (isinstance(g, int) and g == 0):
                    act.wait_ge(accT_ps, g)
                A(accS[:], ACC[:], ACT.Copy).then_inc(acc_saved, 1)

            def chunk(c, g):
                zero = isinstance(g, int) and g == 0
                for u in range(KT // 2):
                    if u == 2 and not zero:
                        sums_move(g - 1)
                    if u == 6 and isinstance(g, int) and g == B * NCH - 1:
                        close_move(0)
                    if u == KT // 2 - 2 and not (isinstance(g, int) and g == B * NCH - 1):
                        max_move(g + 1, RING[PLAN["rows"][0]])
                    act.wait_ge(scores_ready, g * 16 + (u + 1))
                    if u % 2 == 0 and not (zero and u < 4):
                        act.wait_ge(pv_done, g * QUADS + (u // 2 - 1))
                    A(Pb[:, u % 4, :], pairS[u % 2][:], ACT.Exp, scale=1.0 / np.sqrt(XD)).then_inc(exp_done, 1)

            norm_batch_move(1, 0, half[0])
            norm_batch_move(2, 1, half[1])
            kv_move(0, 0)
            act.wait_ge(q_ps, 2)
            A(qraw.rearrange("p (h t) d -> p h t d", t=2),
              bank[0][:].rearrange("p (t h d) -> p h t d", t=2, h=XH), ACT.Copy).then_inc(qraw_done, 1)
            copy = lambda dst, src: A(dst, src, ACT.Copy)

            def k_repeat(n):
                act.wait_ge(k_split, n - 1)
                repeat(copy, kasm[:, n % 2], K_PART).then_inc(k_asm, 1)

            parts_move("q0", "k0", "k1")
            kv_move(0, 1)
            parts_move("q1", "q2", "k2", "k3")
            act.wait_ge(q_split, 1)
            repeat(copy, qasm[:, 2 * XH:4 * XH, :], Q_PART).then_inc(q_asm1, 1)
            kv_move(1, 0)
            parts_move("q3")
            act.wait_ge(v_init, 2 * B)
            kv_rows(1, 0)
            parts_move("q4")
            kv_move(1, 1)
            k_repeat(2)
            parts_move("q5")
            kv_rows(1, 1)
            parts_move("q6", "q7", "k4", "k5")
            k_repeat(3)
            parts_move("k6", "k7")
            max_move(0, ACC)
            for b in range(B):
                chunk(0, b * NCH)
                with act.Fori(0, NCH - 3) as i:
                    chunk(None, i + (b * NCH + 1))
                chunk(NCH - 2, b * NCH + NCH - 2)
                chunk(NCH - 1, b * NCH + NCH - 1)
            sums_move(B * NCH - 1)
            PJ, SB = [half[0], half[1]], [half[2], half[3]]

            def qkv_move(p, par):
                src = [PJ[(3 * par + w) % 2] for w in range(3)]
                bias = lambda w: bqkv[:, w, bass.ds(p, 1)]
                return src, bias

            def q_move(p, par):
                src, bias = qkv_move(p, par)
                act.wait_ge(proj_ps, p * 3 + 1)
                if not (isinstance(p, int) and p < 2):
                    act.wait_ge(s_ps, p * 4 - 4)
                for h in range(2):
                    r = slice(64 * h, 64 * h + 64)
                    last = A(qz[par][r, h, :], src[0][r, :], ACT.Identity, bias=bqkv[r, 0, bass.ds(p, 1)])
                last.then_inc(q_moved, 1)

            def v_move(p, par):
                src, bias = qkv_move(p, par)
                act.wait_ge(proj_ps, p * 3 + 3)
                if not (isinstance(p, int) and p < 1):
                    act.wait_ge(vn_ps, p)
                A(vTb[:], src[2], ACT.Identity, bias=bias(2)).then_inc(v_moved, 1)

            def exps(p, u):
                act.wait_ge(s_max, p * 4 + (u + 1))
                if not (isinstance(p, int) and p == 0):
                    act.wait_ge(pT_ps, p * 4 + (u - 3))
                for hf in range(2):
                    last = A(sp_[:, u, hf * L:(hf + 1) * L], SB[u % 2][:, hf * L:(hf + 1) * L], ACT.Exp,
                             bias=snb[:, u, hf:hf + 1], scale=1.0 / np.sqrt(AD), accum_out=sden[:, u, hf:hf + 1])
                last.then_inc(s_exp, 1)

            def out_move(p, par):
                act.wait_ge(av_ps, p * 2 + 2)
                if not (isinstance(p, int) and p < 2):
                    act.wait_ge(wO_used, p - 1)
                A(aT[par], XB[1][:], ACT.Copy).then_inc(aT_done, 1)

            def high_x(n):
                act.wait_ge(x_cut, n)
                A(xh[:], xc, ACT.Copy).then_inc(x_hi, 1)

            def high_proj(p, par):
                act.wait_ge(wA_cut, p - 1)
                act.wait_ge(proj_ps, p * 3 - 3)
                A(wAh[par][:], wAc[par], ACT.Copy).then_inc(wA_hi, 1)

            def pair(p, par, nxt):
                for u in range(4):
                    if u == 0 and not (isinstance(p, int) and p == 0):
                        out_move(p - 1, 1 - par)
                    if u == 1 and nxt is not None:
                        q_move(p + 1, 1 - par)
                    if u == 3 and nxt is not None:
                        v_move(p + 1, 1 - par)
                    if u < 2:
                        exps(p, u + 2)
                    elif nxt is not None:
                        exps(p + 1, u - 2)
                    if u == 2:
                        if isinstance(p, int) and p == 0:
                            high_x(1)
                        if not (isinstance(p, int) and p + 2 >= NPAIR):
                            high_proj(p + 2, par)

            def q0_move(b):
                for h in range(2):
                    r, cols = slice(64 * h, 64 * h + 64), slice(b * L, (b + 1) * L)
                    last = A(qz[0][r, h, cols], PJ[0][r, cols], ACT.Identity, bias=bqkv[r, 0, 0:1])
                return last

            norm_batch_move(3, 0, bank[1][:])
            act.wait_ge(qz_done, 2)
            act.wait_ge(late_in, 16 * 6)
            act.wait_ge(proj0_ps, 1)
            q0_move(0).then_inc(q0_moved, 1)
            close_move(1)
            norm_batch_move(4, 1, bank[1][:])
            exps(0, 0)
            act.wait_ge(proj_ps, 1)
            q0_move(1).then_inc(q_moved, 1)
            v_move(0, 0)
            exps(0, 1)
            pair(0, 0, 0)
            pair(1, 1, 1)
            with act.Fori(1, NPAIR // 2 - 1) as i:
                pair(i * 2, 0, i)
                pair(i * 2 + 1, 1, i + 1)
            pair(NPAIR - 2, 0, NPAIR // 2 - 1)
            def last_out_move(b):
                act.wait_ge(av_ps, NPAIR * 2 - 1 + b)
                if b == 0:
                    act.wait_ge(wO_used, NPAIR - 2)
                cols = slice(b * L, (b + 1) * L)
                A(aT[1][:, cols], XB[1][:, cols], ACT.Copy).then_inc(aT_done, 1)

            q = NPAIR - 1
            out_move(q - 1, 0)
            exps(q, 2)
            exps(q, 3)
            last_out_move(0)
            last_out_move(1)

            norm_batch_move(5, 0, XB[0][:])
            norm_batch_move(6, 1, XB[1][:])
            GB = [half[0], half[1]]

            def silu(e, par):
                act.wait_ge(up_ps, e + 1)
                if not (isinstance(e, int) and e < 2):
                    act.wait_ge(hT_done, e - 1)
                A(hsil[par], GB[par], ACT.Silu).then_inc(sil_done, 1)

            def high(dst, cut, e, cut_done, used, done):
                act.wait_ge(cut_done, e - 1)
                if not (isinstance(e, int) and e < 4):
                    act.wait_ge(used, e - 1)
                A(dst, cut, ACT.Copy).then_inc(done, 1)

            def high_up(e, par):
                high(wUh[par], wUc[par], e, wU_cut, up_ps, wU_hi)

            def high_down(e, par):
                high(wDh[par][:], wDc[par], e, wD_cut, down_ps, wD_hi)

            def high_hidden(e, par):
                high(hh[par][:], hc[par], e, hT_cut, down_ps, hT_hi)

            silu(0, 0)
            act.wait_ge(gate_ps, 1)
            A(Pb[:, 3, 0:T * E], ACC[:, 0:T * E], ACT.Exp, scale=-1.0).then_inc(gate_exp, 1)
            high_x(2)
            high_up(2, 0)
            silu(1, 1)
            high_up(3, 1)
            high_down(2, 0)
            silu(2, 0)
            high_hidden(2, 0)
            high_up(4, 0)
            high_down(3, 1)
            silu(3, 1)
            high_hidden(3, 1)
            high_up(5, 1)

            def turn(e):
                for par in range(2):
                    high_down(e + (2 + par), par)
                    silu(e + (2 + par), par)
                    high_hidden(e + (2 + par), par)
                    if not (isinstance(e, int) and e + 4 >= NE):
                        high_up(e + (4 + par), par)

            with act.Fori(1, NE // 2 - 2) as i:
                turn(i * 2)
            turn(NE - 4)

        @block.vector
        def _(dve):
            ch = Chain(dve, dve_chain)
            TT, TS, CP = nc.vector.tensor_tensor, nc.vector.tensor_scalar, nc.vector.tensor_copy
            STT = nc.vector.scalar_tensor_tensor

            def layer_norm(tiles=range(T)):
                c = slice(tiles[0], tiles[-1] + 1)
                for t in tiles:
                    ins = nc.vector.bn_stats(st6[:, t, :], xs[:, t, :])
                ch.step(ins)
                for t in tiles:
                    ins = nc.vector.bn_aggr(mv[:, t, :], st6[:, t, :])
                ch.step(ins)
                ch.step(TS(rv[:, c], mv[:, c, 1], EPS, None, ALU.add))
                ch.step(TS(ry[:, c].bitcast(I32), rv[:, c].bitcast(I32), -0.5, RSQRT_MAGIC, ALU.mult, ALU.add))
                for _ in range(3):
                    ch.step(TT(rt[:, c], ry[:, c], ry[:, c], ALU.mult))
                    ch.step(STT(out=rt[:, c], in0=rt[:, c], scalar=-0.5, in1=rv[:, c], op0=ALU.mult, op1=ALU.mult))
                    ch.step(STT(out=ry[:, c], in0=rt[:, c], scalar=1.5, in1=ry[:, c], op0=ALU.add, op1=ALU.mult))
                for t in tiles:
                    ins = TS(xn[:, t, :], xs[:, t, :], mv[:, t, 0:1], ry[:, t:t + 1], ALU.subtract, ALU.mult)
                ins.then_inc(ln_done, 1)

            def add_batch(b, src):
                flat = xs[:].rearrange("p t d -> p (t d)")[:, b * 512:(b + 1) * 512]
                ch.step(TT(flat, src, flat, ALU.add))

            def close(b):
                dve.wait_ge(y_ps, b + 1)
                add_batch(b, MISC[:])
                layer_norm(range(2 * b, 2 * b + 2))

            def kv_rows(b, s):
                n = 2 * b + s
                dve.wait_ge(kn_ps, n + 1)
                nat = half[3].rearrange("p (t j c) -> p j t c", t=4, j=4)
                tiles = V[b][:, s * 16:(s + 1) * 16, :].rearrange("p (j t) c -> p j t c", t=4)
                CP(kraw[:, n % 2].rearrange("p (j t) c -> p j t c", t=4), nat[:, :, :, 0:XD])
                CP(tiles[:, :, :, 0:XD], nat[:, :, :, XD:2 * XD]).then_inc(kn_read, 1)
                dve.wait_ge(kn_read, n + 1)
                ch.step(split(TT, CP, ch, kraw[:, n % 2], kasm[:, n % 2], resv, KT // 2, K_PART))
                repeat(CP, kasm[:, n % 2], K_PART).then_inc(k_asm, 1)

            def row_max(dst, src):
                nc.vector.reduce_max(dst, src[:], AX).then_inc(xmax_read, 1)

            def first_items(w0, w1):
                for w in range(w0, w1):
                    dve.wait_ge(xmax_ready, w + 1)
                    blk, k = first_item(w)
                    row_max(mxp[:, blk % NBLK, k:k + 1], RING[first_bank(w)])

            def max_item(j, g, c):
                ahead = AHEAD + j // KC
                if g is None or not isinstance(g, int) or g * NBLK + ahead < B * NCH * NBLK:
                    dve.wait_ge(xmax_ready, g * NITEM + (AHEAD * KC + j + 1))
                    row_max(mxp[:, ahead % NBLK, j % KC:j % KC + 1], RING[PLAN[j][0]])

            def block_max(n, w):
                dve.wait_ge(xmax_read, w)
                if not (isinstance(n, int) and n == 0):
                    dve.wait_ge(mparts_ready, n)
                nc.vector.reduce_max(mmax[:], mxp[:], AX).then_inc(mmax_ready, 1)
                dve.wait_ge(mmax_ready, n + 1)

            def sums_rows(g):
                dve.wait_ge(accT_ps, g + 1)
                if not (isinstance(g, int) and g == 0):
                    dve.wait_ge(o_done, g)
                sums = RING[PLAN["sums"][0]][:].rearrange("p (i k c) -> p i c k", i=NBLK, k=4)
                nc.vector.reduce_sum(osum[:], sums[:, :, 0:XD + 1, :], AX).then_inc(accT_read, 1)
                dve.wait_ge(accT_read, g + 1)
                nc.vector.reciprocal(oden[:], osum[:, :, XD]).then_inc(osum_ready, 1)

            def chunk(g):
                for v in range(QUADS):
                    for j in range(4):
                        max_item(4 * v + j, g, None)
                    if v == 2 and not (isinstance(g, int) and g == 0):
                        sums_rows(g - 1)
                    if v == 5 and not (isinstance(g, int) and g == B * NCH - 1):
                        block_max(g + 1, g * NITEM + (AHEAD * KC + 24))

            for b in range(B):
                nc.vector.memset(V[b][:], 0.0).then_inc(v_init, 1)
                dve.wait_ge(v_init, 2 * b + 1)
                nc.vector.memset(V[b][:, :, XD:XD + 1], 1.0).then_inc(v_init, 1)
            dve.wait_ge(x_in, 16)
            layer_norm(range(0, 2))
            layer_norm(range(2, 4))
            dve.wait_ge(q_ps, 1)
            ch.step(split(TT, CP, ch, ACC[:].rearrange("p (t h d) -> p h t d", t=2, h=XH), qasm[:, 0:2 * XH, :], resv,
                          2 * XH, Q_PART, view=lambda ap: ap.rearrange("p (h t) d -> p h t d", t=2)))
            repeat(CP, qasm[:, 0:2 * XH, :], Q_PART).then_inc(q_asm0, 1)
            dve.wait_ge(v_init, 2 * B)
            kv_rows(0, 0)
            first_items(0, 6)
            kv_rows(0, 1)
            first_items(6, NBLK * KC)
            block_max(0, NBLK * KC)
            first_items(NBLK * KC, AHEAD * KC)
            for b in range(B):
                chunk(b * NCH)
                with dve.Fori(0, NCH - 3) as i:
                    chunk(i + (b * NCH + 1))
                chunk(b * NCH + NCH - 2)
                chunk(b * NCH + NCH - 1)
            close(0)
            sums_rows(B * NCH - 1)

            PJ, SB = [half[0], half[1]], [half[2], half[3]]

            def cut(dst, src):
                return TS(dst.bitcast(I32), src.bitcast(I32), HIGH_BITS, None, ALU.bitwise_and)

            def cut_x():
                cut(xc, xnT[:]).then_inc(x_cut, 1)

            def cut_proj(p, par, turn):
                dve.wait_ge(wA_in[par], turn * 16 + 16)
                if not (isinstance(p, int) and p < 4):
                    dve.wait_ge(wA_hi, p - 3)
                    dve.wait_ge(wA_lo, p - 3)
                cut(wAc[par], wA[par][:]).then_inc(wA_cut, 1)

            def k_move(p, par):
                dve.wait_ge(proj_ps, p * 3 + 2)
                if not (isinstance(p, int) and p < 2):
                    dve.wait_ge(s_ps, p * 4 - 4)
                TS(kTb[par][:], PJ[(3 * par + 1) % 2], bqkv[:, 1, bass.ds(p, 1)], None, ALU.add).then_inc(k_moved, 1)

            def v_rows(p, par):
                dve.wait_ge(vn_ps, p + 1)
                if not (isinstance(p, int) and p < 2):
                    dve.wait_ge(av_ps, p * 2 - 2)
                CP(vn[par][:].rearrange("p t n -> p (t n)"), PJ[(3 * par + 2) % 2]).then_inc(vn_done, 1)

            def row_max(p, u):
                dve.wait_ge(s_ps, p * 4 + (u + 1))
                ch.step(nc.vector.reduce_max(smx[:, u, :], SB[u % 2].rearrange("p (h k) -> p h k", h=2), AX))
                TS(snb[:, u, :], smx[:, u, :], -1.0 / np.sqrt(AD), None, ALU.mult).then_inc(s_max, 1)

            def normalize(p, u):
                dve.wait_ge(s_exp, p * 4 + (u + 1))
                ch.step(nc.vector.reciprocal(srd[:, u, :], sden[:, u, :]))
                for hf in range(2):
                    w = sp_[:, u, hf * L:(hf + 1) * L]
                    ins = TS(w, w, srd[:, u, hf:hf + 1], None, ALU.mult)
                ins.then_inc(s_norm, 1)

            def pT_move(p, u):
                dve.wait_ge(pT_ps, p * 4 + (u + 1))
                if u >= 2 or not (isinstance(p, int) and p == 0):
                    dve.wait_ge(av_ps, p * 2 + u // 2)
                CP(spT[:, u % 2, :], XB[0][:]).then_inc(pT_done, 1)

            def pair(p, par, nxt):
                for u in range(4):
                    if u == 0:
                        v_rows(p, par)
                    if u == 2 and nxt is not None:
                        k_move(p + 1, 1 - par)
                    pT_move(p, u)
                    if u < 3:
                        normalize(p, u + 1)
                    elif nxt is not None:
                        normalize(p + 1, 0)
                    if u < 2:
                        row_max(p, u + 2)
                    elif nxt is not None:
                        row_max(p + 1, u - 2)
                    if u == 2:
                        if isinstance(p, int) and p == 0:
                            dve.wait_ge(xnT_done, 4)
                            cut_x()
                        if not (isinstance(p, int) and p + 2 >= NPAIR):
                            cut_proj(p + 2, par, nxt + (1 - par))

            def k0_move(b):
                cols = slice(b * L, (b + 1) * L)
                return TS(kTb[0][:, cols], PJ[1][:, cols], bqkv[:, 1, 0:1], None, ALU.add)

            dve.wait_ge(late_in, 16 * 6)
            dve.wait_ge(proj0_ps, 2)
            k0_move(0).then_inc(k0_moved, 1)
            close(1)
            row_max(0, 0)
            normalize(0, 0)
            dve.wait_ge(proj_ps, 2)
            k0_move(1).then_inc(k_moved, 1)
            row_max(0, 1)
            pair(0, 0, 0)
            pair(1, 1, 1)
            with dve.Fori(1, NPAIR // 2 - 1) as i:
                ch.loop(i - 1, 16)
                pair(i * 2, 0, i)
                pair(i * 2 + 1, 1, i + 1)
                ch.end(NPAIR // 2 - 2)
            pair(NPAIR - 2, 0, NPAIR // 2 - 1)
            q = NPAIR - 1
            v_rows(q, 1)
            pT_move(q, 0)
            normalize(q, 1)
            row_max(q, 2)
            pT_move(q, 1)
            normalize(q, 2)
            row_max(q, 3)
            pT_move(q, 2)
            normalize(q, 3)
            dve.wait_ge(wO_used, NPAIR)
            add_batch(0, ACC[:])
            pT_move(q, 3)
            layer_norm(range(0, 2))
            dve.wait_ge(wO_used, NPAIR + 1)
            add_batch(1, MISC[:])
            layer_norm(range(2, 4))
            dve.wait_ge(ln_done, 6)
            ch.step(TT(xs[:], xs[:], xn[:], ALU.add))

            UB, DB = [half[2], half[3]], [XB, [ACC, MISC]]

            def hidden(e, par):
                dve.wait_ge(sil_done, e + 1)
                if isinstance(e, int) and 2 <= e < 4:
                    dve.wait_ge(down_ps, e - 1)
                elif not (isinstance(e, int) and e < 2):
                    dve.wait_ge(hT_hi, e - 3)
                    dve.wait_ge(hT_lo, e - 3)
                TT(hT[par], UB[par], hsil[par], ALU.mult).then_inc(hT_done, 1)
                if not (isinstance(e, int) and e < 2):
                    dve.wait_ge(hT_done, e + 1)
                    cut(hc[par], hT[par]).then_inc(hT_cut, 1)

            def cut_up(e, par, turn):
                dve.wait_ge(wU_in[par], turn * 16 + 16)
                if not (isinstance(e, int) and e < 4):
                    dve.wait_ge(wU_hi, e - 3)
                    dve.wait_ge(wU_lo, e - 3)
                cut(wUc[par], wU[par][:]).then_inc(wU_cut, 1)

            def cut_down(e, par, turn):
                dve.wait_ge(wD_in[par], turn * 16 + 16)
                if not (isinstance(e, int) and e < 4):
                    dve.wait_ge(wD_hi, e - 3)
                    dve.wait_ge(wD_lo, e - 3)
                cut(wDc[par], wD[par][:]).then_inc(wD_cut, 1)

            def add_expert(e, par, cw_e):
                dve.wait_ge(down_ps, e + 1)
                for t in range(T):
                    ins = nc.vector.scalar_tensor_tensor(out=xs[:, t, :], in0=DB[par][t // 2][:, (t % 2) * D:(t % 2 + 1) * D],
                                                         scalar=cw[:, t, cw_e], in1=xs[:, t, :], op0=ALU.mult, op1=ALU.add)
                    if t % 2:
                        ins.then_inc(down_read, 1)
                return ins

            dve.wait_ge(xnT_done, 6)
            cut_x()
            hidden(0, 0)
            cut_up(2, 0, 1)

            tmp = lambda i, n: Pb[:, 3, 64 + i:64 + i + n]
            sg = Pb[:, 3, 0:64]
            sfc = Pb[:, 3, 64:128]
            dve.wait_ge(gate_exp, 1)
            ch.step(TS(sg, sg, 1.0, None, ALU.add))
            ch.step(nc.vector.reciprocal(sg, sg))
            s3 = sg.rearrange("p (t e) -> p t e", t=T)
            c3 = sfc.rearrange("p (t e) -> p t e", t=T)
            ch.step(TT(c3, s3, gb[:].unsqueeze(1).broadcast_to([P, T, E]), ALU.add))
            c4 = sfc.rearrange("p (n a b) -> p n a b", a=2, b=2)
            hi = Pb[:, 3, 128:160].rearrange("p (n a) -> p n a", a=2)
            lo = Pb[:, 3, 160:192].rearrange("p (n a) -> p n a", a=2)
            TT(hi, c4[:, :, :, 0], c4[:, :, :, 1], ALU.max)
            ch.step(TT(lo, c4[:, :, :, 0], c4[:, :, :, 1], ALU.min))
            gs = Pb[:, 3, 192:208]
            g2 = Pb[:, 3, 208:240].rearrange("p (n a) -> p n a", a=2)
            TT(gs, hi[:, :, 0], hi[:, :, 1], ALU.add)
            ch.step(TT(g2, hi, lo, ALU.add))
            ch.step(TT(gs, gs, g2[:, :, 0], ALU.max))
            ch.step(TT(gs, gs, g2[:, :, 1], ALU.max))
            def ranks(vals, n, pair_cmp, rank):
                cmp4 = pair_cmp.rearrange("p (t i j) -> p t i j", t=T, i=n)
                for i in range(n):
                    me = vals[:, :, i:i + 1]
                    if i:
                        ins = TT(cmp4[:, :, i, 0:i], vals[:, :, 0:i], me.broadcast_to([P, T, i]), ALU.is_ge)
                    ins = TT(cmp4[:, :, i, i:n], vals[:, :, i:n], me.broadcast_to([P, T, n - i]), ALU.is_gt)
                ch.step(ins)
                ch.step(nc.vector.reduce_sum(rank, cmp4, AX))

            gr = Pb[:, 3, 240:256].rearrange("p (t g) -> p t g", t=T)
            ranks(gs.rearrange("p (t g) -> p t g", t=T), NG, Pb[:, 3, 256:320], gr)
            ch.step(TS(gr, gr, float(TG) - 0.5, None, ALU.is_lt))
            mk = Pb[:, 3, 320:384]
            mk4 = mk.rearrange("p (n e) -> p n e", e=E // NG)
            grb = Pb[:, 3, 240:256].unsqueeze(2).broadcast_to([P, T * NG, E // NG])
            ch.step(TT(mk4, sfc.rearrange("p (n e) -> p n e", e=E // NG), grb, ALU.mult))
            pen = Pb[:, 3, 384:400]
            ch.step(TS(pen, Pb[:, 3, 240:256], -1.0, BIG, ALU.add, ALU.mult))
            ch.step(TT(mk4, mk4, pen.unsqueeze(2).broadcast_to([P, T * NG, E // NG]), ALU.add))
            hidden(1, 1)
            cut_up(3, 1, 1)
            cut_down(2, 0, 1)
            add_expert(0, 0, slice(0, 1))
            hidden(2, 0)
            cut_up(4, 0, 2)
            cut_down(3, 1, 1)
            er = Pb[:, 3, 400:464].rearrange("p (t e) -> p t e", t=T)
            mk3 = mk.rearrange("p (t e) -> p t e", t=T)
            best = Pb[:, 2, 0:8 * T].rearrange("p (t n) -> p t n", t=T)
            for t in range(T):
                ins = nc.vector.max(best[:, t, :], mk3[:, t, :])
            ch.step(ins)
            ch.step(nc.vector.memset(best[:, :, TOPK:8], BIG))
            for t in range(T):
                ins = nc.vector.match_replace(er[:, t, :], best[:, t, :], mk3[:, t, :], BIG)
            ch.step(ins)
            dve.wait_ge(down_read, 2)
            add_expert(1, 1, slice(1, 2))
            hidden(3, 1)
            cut_up(5, 1, 2)
            ch.step(TT(er, er, mk3, ALU.not_equal))
            ch.step(TT(er, er, s3, ALU.mult))
            den = Pb[:, 3, 464:468]
            ch.step(nc.vector.reduce_sum(den, er, AX))
            ch.step(TS(den, den, 1e-20, None, ALU.add))
            ch.step(nc.vector.reciprocal(den, den))
            ch.step(TT(er, er, den.unsqueeze(2).broadcast_to([P, T, E]), ALU.mult))
            ch.step(TS(cw[:, :, 2:NE], er, 2.5, None, ALU.mult))

            def turn(i, e):
                for par in range(2):
                    cut_down(e + (2 + par), par, i + 1)
                    dve.wait_ge(down_read, e * 2 + 2 * par)
                    add_expert(e + par, par, bass.ds(e + par, 1))
                    hidden(e + (2 + par), par)
                    if not (isinstance(e, int) and e + 4 >= NE):
                        cut_up(e + (4 + par), par, i + 2)

            with dve.Fori(1, NE // 2 - 2) as i:
                turn(i, i * 2)
            turn(NE // 2 - 2, NE - 4)
            dve.wait_ge(down_read, 2 * NE - 4)
            add_expert(NE - 2, 0, slice(NE - 2, NE - 1))
            dve.wait_ge(down_read, 2 * NE - 2)
            add_expert(NE - 1, 1, slice(NE - 1, NE))



def kernel(x, ctx_1024, L0_xattn_w_q, L0_xattn_w_kv, L0_xattn_w_concat, L0_attn_W_qkv, L0_attn_b_qkv, L0_attn_W_out,
           L0_attn_b_out, L0_ffn_gate_w, L0_ffn_gate_bias, L0_ffn_Wg, L0_ffn_Wu, L0_ffn_Wd, L0_ffn_Ws_g, L0_ffn_Ws_u,
           L0_ffn_Ws_d):
    import concourse.bacc as bacc
    from concourse.bass_utils import run_bass_kernel_spmd

    a = np.asarray
    wqkv = a(L0_attn_W_qkv).reshape(KD, P, 3, NPAIR, P).transpose(3, 1, 0, 2, 4).reshape(NPAIR, P, KD * 3 * P)
    wout = a(L0_attn_W_out).reshape(NPAIR, P, D)
    bqkv = a(L0_attn_b_qkv).reshape(3, NPAIR, P).transpose(2, 0, 1)

    def up(w):
        return a(w).reshape(-1, I, KD, P).transpose(0, 3, 2, 1)

    def gate_up(g, u):
        return np.stack([up(g), up(u)], axis=3).reshape(-1, P, KD * 2 * I)

    shared_d = a(L0_ffn_Ws_d).T.reshape(2, P, D)
    w_up = np.concatenate([gate_up(L0_ffn_Ws_g, L0_ffn_Ws_u), gate_up(L0_ffn_Wg, L0_ffn_Wu)], axis=0)
    w_down = np.concatenate([shared_d, a(L0_ffn_Wd).transpose(0, 2, 1)], axis=0)
    arrays = {
        "x": a(x),
        "ctxT": a(ctx_1024).transpose(0, 2, 1),
        "w_q": a(L0_xattn_w_q), "w_kv": a(L0_xattn_w_kv), "w_cat": a(L0_xattn_w_concat),
        "w_qkv": wqkv, "b_qkv": bqkv, "w_out": wout, "b_out": a(L0_attn_b_out),
        "gate_wT": a(L0_ffn_gate_w).T, "gate_b": a(L0_ffn_gate_bias),
        "w_up": w_up, "w_down": w_down,
    }
    arrays = {k: np.ascontiguousarray(v) for k, v in arrays.items()}
    nc = bacc.Bacc("TRN2", target_bir_lowering=False, num_devices=1)
    args = [nc.dram_tensor(k, v.shape, mybir.dt.from_np(v.dtype), kind="ExternalInput").ap()
            for k, v in arrays.items()]
    args.append(nc.dram_tensor("out", (B, L, D), F32, kind="ExternalOutput").ap())
    build(nc, *args)
    r = run_bass_kernel_spmd(nc, [arrays], core_ids=[0])
    return r.results[0]["out"]
```
